# Optimizing a Trainium2 kernel written in Bass

```python
import numpy as np
import jax
import jax.numpy as jnp

def _softmax(x, axis=-1):
    return jax.nn.softmax(x, axis=axis)

def _gelu(x):
    return jax.nn.gelu(x, approximate=True)

def _silu(x):
    return jax.nn.silu(x)

def _sigmoid(x):
    return jax.nn.sigmoid(x)

def _layernorm(x, axis=-1, eps=1e-05):
    m = jnp.mean(x, axis=axis, keepdims=True)
    v = jnp.var(x, axis=axis, keepdims=True)
    return (x - m) / jnp.sqrt(v + eps)

def _scatter_add(tgt, idx, src, axis=0):
    return tgt.at[idx].add(src)

def _segment_sum(src, seg, n):
    return jax.ops.segment_sum(src, seg, n)
kernel_name = 'mk_prb_d2_jaxref_r8_802b27'

def setup_inputs(seed: int=0):
    np.random.seed(seed)
    _w = jnp.asarray

    def _L0_attn_setup():
        import jax, jax.numpy as jnp
        import numpy as np
        B, T, D = (1, 256, 512)
        H, G = (32, 8)
        HD = D // H
        REP = H // G
        KV_DIM = 2 * HD * G
        key = jax.random.key(seed)
        k0, k1, k2, k3 = jax.random.split(key, 4)
        x = jax.random.normal(k0, (B, T, D), dtype=jnp.float32)
        Wq = jax.random.normal(k1, (D, D), dtype=jnp.float32) * 0.02
        Wkv = jax.random.normal(k2, (D, KV_DIM), dtype=jnp.float32) * 0.02
        Wo = jax.random.normal(k3, (D, D), dtype=jnp.float32) * 0.02
        bo = jnp.zeros((D,), dtype=jnp.float32)
        return {'x': x, 'Wq': Wq, 'Wkv': Wkv, 'Wo': Wo, 'bo': bo}
    _L0_attn_in = _L0_attn_setup()

    def _L0_ffn_setup():
        import jax, jax.numpy as jnp
        import numpy as np
        RMS_EPS = 1e-05
        key = jax.random.key(seed)
        k1, k2, k3, k4 = jax.random.split(key, 4)
        B, S, H, I = (1, 256, 512, 1792)
        x = jax.random.normal(k1, (B, S, H), dtype=jnp.float32)
        ln_w = jnp.ones((H,), dtype=jnp.float32)
        gate_w = jax.random.normal(k2, (I, H), dtype=jnp.float32) * 0.02
        up_w = jax.random.normal(k3, (I, H), dtype=jnp.float32) * 0.02
        down_w = jax.random.normal(k4, (H, I), dtype=jnp.float32) * 0.02
        return {'x': x, 'ln_w': ln_w, 'gate_w': gate_w, 'up_w': up_w, 'down_w': down_w}
    _L0_ffn_in = _L0_ffn_setup()

    def _L1_attn_setup():
        import jax, jax.numpy as jnp
        import numpy as np
        import math
        B, L, D, H = (32, 64, 512, 32)
        HD = D // H
        key = jax.random.key(seed)
        ks = jax.random.split(key, 9)
        s = 1.0 / math.sqrt(D)
        return {'x': jax.random.normal(ks[0], (B, L, D), jnp.float32), 'Wq': jax.random.normal(ks[1], (D, D), jnp.float32) * s, 'bq': jax.random.normal(ks[2], (D,), jnp.float32) * s, 'Wk': jax.random.normal(ks[3], (D, D), jnp.float32) * s, 'bk': jax.random.normal(ks[4], (D,), jnp.float32) * s, 'Wv': jax.random.normal(ks[5], (D, D), jnp.float32) * s, 'bv': jax.random.normal(ks[6], (D,), jnp.float32) * s, 'Wo': jax.random.normal(ks[7], (D, D), jnp.float32) * s, 'bo': jax.random.normal(ks[8], (D,), jnp.float32) * s}
    _L1_attn_in = _L1_attn_setup()

    def _L1_ffn_setup():
        import jax, jax.numpy as jnp
        import numpy as np
        D_MODEL = 512
        D_FF = 1376
        key = jax.random.key(seed)
        k1, k2, k3, k4 = jax.random.split(key, 4)
        x = jax.random.normal(k1, (2, 256, D_MODEL), dtype=jnp.float32)
        W_gate = jax.random.normal(k2, (D_FF, D_MODEL), dtype=jnp.float32) * D_MODEL ** (-0.5)
        W_up = jax.random.normal(k3, (D_FF, D_MODEL), dtype=jnp.float32) * D_MODEL ** (-0.5)
        W_down = jax.random.normal(k4, (D_MODEL, D_FF), dtype=jnp.float32) * D_FF ** (-0.5)
        return {'x': x, 'W_gate': W_gate, 'W_up': W_up, 'W_down': W_down}
    _L1_ffn_in = _L1_ffn_setup()
    _d = {'L0_attn_x': _L0_attn_in['x'], 'L0_attn_Wq': _L0_attn_in['Wq'], 'L0_attn_Wkv': _L0_attn_in['Wkv'], 'L0_attn_Wo': _L0_attn_in['Wo'], 'L0_attn_bo': _L0_attn_in['bo'], 'L0_ffn_ln_w': _L0_ffn_in['ln_w'], 'L0_ffn_gate_w': _L0_ffn_in['gate_w'], 'L0_ffn_up_w': _L0_ffn_in['up_w'], 'L0_ffn_down_w': _L0_ffn_in['down_w'], 'L1_attn_Wq': _L1_attn_in['Wq'], 'L1_attn_bq': _L1_attn_in['bq'], 'L1_attn_Wk': _L1_attn_in['Wk'], 'L1_attn_bk': _L1_attn_in['bk'], 'L1_attn_Wv': _L1_attn_in['Wv'], 'L1_attn_bv': _L1_attn_in['bv'], 'L1_attn_Wo': _L1_attn_in['Wo'], 'L1_attn_bo': _L1_attn_in['bo'], 'L1_ffn_W_gate': _L1_ffn_in['W_gate'], 'L1_ffn_W_up': _L1_ffn_in['W_up'], 'L1_ffn_W_down': _L1_ffn_in['W_down']}
    _x0 = _d['L0_attn_x']
    _d['L0_attn_x'] = jax.random.normal(jax.random.fold_in(jax.random.key(seed), 1), (2, 512, 512), dtype=_x0.dtype)
    del _x0
    return _d

def reference(L0_attn_x, L0_attn_Wq, L0_attn_Wkv, L0_attn_Wo, L0_attn_bo, L0_ffn_ln_w, L0_ffn_gate_w, L0_ffn_up_w, L0_ffn_down_w, L1_attn_Wq, L1_attn_bq, L1_attn_Wk, L1_attn_bk, L1_attn_Wv, L1_attn_bv, L1_attn_Wo, L1_attn_bo, L1_ffn_W_gate, L1_ffn_W_up, L1_ffn_W_down):

    def _L0_attn_ref(x, Wq, Wkv, Wo, bo):
        import jax, jax.numpy as jnp
        import numpy as np
        B, T, D = (1, 256, 512)
        H, G = (32, 8)
        HD = D // H
        REP = H // G
        KV_DIM = 2 * HD * G
        b, t, d = x.shape
        q = jnp.dot(x, Wq).reshape(b, t, H, HD).transpose(0, 2, 1, 3)
        kv = jnp.dot(x, Wkv).reshape(b, t, G, 2, HD).transpose(2, 3, 0, 1, 4)
        k, v = (kv[:, 0], kv[:, 1])
        k = jnp.broadcast_to(k[:, :, None], (G, b, REP, t, HD)).reshape(b, H, t, HD)
        v = jnp.broadcast_to(v[:, :, None], (G, b, REP, t, HD)).reshape(b, H, t, HD)
        scores = jnp.einsum('bhqd,bhkd->bhqk', q, k)
        causal = jnp.triu(jnp.ones((t, t), dtype=bool), 1)
        scores = jnp.where(causal[None, None], -jnp.inf, scores)
        weights = jax.nn.softmax(scores * (1.0 / HD ** 0.5), axis=-1)
        ctx = jnp.einsum('bhqk,bhkd->bhqd', weights, v)
        ctx = ctx.transpose(0, 2, 1, 3).reshape(b, t, d)
        return jnp.dot(ctx, Wo) + bo

    def _L0_ffn_ref(x, ln_w, gate_w, up_w, down_w):
        import jax, jax.numpy as jnp
        import numpy as np
        RMS_EPS = 1e-05
        var = jnp.mean(jnp.square(x), axis=-1, keepdims=True)
        nx = x * jax.lax.rsqrt(var + RMS_EPS) * ln_w
        g = jnp.einsum('bsh,ih->bsi', nx, gate_w)
        u = jnp.einsum('bsh,ih->bsi', nx, up_w)
        return jnp.einsum('bsi,hi->bsh', jax.nn.silu(g) * u, down_w)

    def _L1_attn_ref(x, Wq, bq, Wk, bk, Wv, bv, Wo, bo):
        import jax, jax.numpy as jnp
        import numpy as np
        import math
        B, L, D, H = (32, 64, 512, 32)
        HD = D // H
        b, l, d = x.shape
        h, hd = (H, HD)
        q = (x @ Wq.T + bq).reshape(b, l, h, hd).transpose(0, 2, 1, 3)
        k = (x @ Wk.T + bk).reshape(b, l, h, hd).transpose(0, 2, 1, 3)
        v = (x @ Wv.T + bv).reshape(b, l, h, hd).transpose(0, 2, 1, 3)
        scores = jnp.einsum('bhqd,bhkd->bhqk', q, k) / math.sqrt(hd)
        causal = jnp.tril(jnp.ones((l, l), bool))
        scores = jnp.where(causal, scores, -jnp.inf)
        att = jax.nn.softmax(scores, axis=-1)
        out = jnp.einsum('bhqk,bhkd->bhqd', att, v)
        out = out.transpose(0, 2, 1, 3).reshape(b, l, d)
        return out @ Wo.T + bo

    def _L1_ffn_ref(x, W_gate, W_up, W_down):
        import jax, jax.numpy as jnp
        import numpy as np
        D_MODEL = 512
        D_FF = 1376
        out_shape = x.shape[:-1] + (W_down.shape[0],)
        xf = x.reshape(-1, x.shape[-1])
        up = jnp.einsum('td,fd->tf', xf, W_up)
        gate = jax.nn.silu(jnp.einsum('td,fd->tf', xf, W_gate))
        h = gate * up
        y = jnp.einsum('tf,df->td', h, W_down)
        return y.reshape(out_shape)
    x = L0_attn_x
    xn = _layernorm(x, axis=-1)
    x = x + _L0_attn_ref(xn, L0_attn_Wq, L0_attn_Wkv, L0_attn_Wo, L0_attn_bo) + _L0_ffn_ref(xn, L0_ffn_ln_w, L0_ffn_gate_w, L0_ffn_up_w, L0_ffn_down_w)
    xn = _layernorm(x, axis=-1)
    x = x + _L1_attn_ref(xn, L1_attn_Wq, L1_attn_bq, L1_attn_Wk, L1_attn_bk, L1_attn_Wv, L1_attn_bv, L1_attn_Wo, L1_attn_bo) + _L1_ffn_ref(xn, L1_ffn_W_gate, L1_ffn_W_up, L1_ffn_W_down)
    return x

_drawn_inputs = setup_inputs


def setup_inputs(seed=0):
    import zlib

    import numpy as np

    out = dict(_drawn_inputs(seed))
    spreads = {'L0_attn_bo': (0.0, 0.1), 'L0_ffn_ln_w': (1.0, 0.2)}
    factors = {'L0_attn_Wq': 8.0, 'L1_attn_bq': 8.0, 'L1_attn_bk': 8.0}
    for name, (base, spread) in spreads.items():
        noise = np.random.default_rng([zlib.crc32(name.encode()), seed]).standard_normal(out[name].shape)
        drawn = base * np.exp(spread * noise) if base else spread * noise
        out[name] = jnp.asarray(drawn.astype(out[name].dtype))
    for name, factor in factors.items():
        out[name] = (out[name] * factor).astype(out[name].dtype)
    return out
```

```python
from contextlib import ExitStack

import numpy as np
import concourse.bass as bass
from concourse import mybir

F32 = mybir.dt.float32
F32R = mybir.dt.float32r
BF16 = mybir.dt.bfloat16
F16 = mybir.dt.float16
ALU = mybir.AluOpType
ACT = mybir.ActivationFunctionType
AX = mybir.AxisListType.X

P = 128
B, T, D = 2, 512, 512
H, G, HD = 32, 8, 16
REP = H // G
KT = D // P
TT = T // P
FF = (1792, 1376)
FT = tuple(-(-f // P) for f in FF)
PAIRS = H // 2
SLOTS = PAIRS
PHASES = ((0, 0), (0, 1), (1, 0), (1, 1))
HALF = D // 2
VW = 50
QROWS = 6 * HD
MROWS = QROWS + 3
Q_PARTS = (0, 0, 1, 0, 1, 2)
K_PARTS = (0, 1, 0, 2, 1, 0)
SCALE = 1.0 / HD ** 0.5
EPS = 1e-5
LOWEST = -3.0e38

RAW, SPLIT, HSPLIT, PRING, SRING = 2, 3, 3, 6, 3


def chunk_table():
    names = []
    for l in range(2):
        names += [("q", l, m) for m in range(4)]
        names += [("k", l, m) for m in range(1 if l == 0 else 4)]
        names += [("v", l, m) for m in range(1 if l == 0 else 4)]
        for f in range(FT[l]):
            names += [("g", l, f), ("u", l, f)]
        names += [("o", l, nh, c) for nh in range(2) for c in range(2)]
        names += [("d", l, nh, c) for nh in range(2) for c in range(-(-FT[l] // 2))]
    return {n: i for i, n in enumerate(names)}


def plan():
    line = {"pe": [], "act": [], "dve": [], "pool": [], "sp": []}
    table = chunk_table()
    state = {"t": 0.0, "chunk": 0, "g": 0, "acc": 0, "ring": 0, "qk": 0, "hs": 0, "tj": 0, "gate": 0}
    chunk_end, split_key, load_key, hs_end = [], [], [], []

    due_at = {}

    def put(engine, key, *step):
        line[engine].append((key, len(line[engine]), step))
        return key

    def not_before(*names):
        for name in names:
            state["t"] = max(state["t"], due_at.get(name, -1e9) + 0.01)

    def take(name):
        state[name] += 1
        return state[name] - 1

    def chunk(name, cost):
        c, now = take("chunk"), state["t"]
        split_early = chunk_end[c - SPLIT] + 0.61 if c >= SPLIT else -1e9
        state["t"] = now = max(now, split_early + 0.02)
        s = max(now - 5.0, chunk_end[c - SPLIT] + 0.61 if c >= SPLIT else -1e9)
        w = max(now - 11.0, split_key[c - RAW] + 0.7 if c >= RAW else -1e9)
        s = max(s, w + 2.0)
        split_key.append(s)
        state["t"] = now = max(now, s + 0.02)
        load_key.append(w)
        chunk_end.append(now + cost)
        put("act", s - 0.6, "whi", c)
        put("pool", s, "wlo", c)
        put("act", w, "wload", c, table[name])
        return c

    def advance(cost):
        state["t"] += cost
        return state["t"]

    def ln_stats(l, b):
        not_before(("xbias", l - 1, b))
        t = state["t"]
        for i, (eng, what) in enumerate((("dve", "stats"), ("act", "root"), ("dve", "rstd"))):
            put(eng, t + 0.1 * i, what, l, b)
        if l == 0:
            put("act", t + 0.3, "root2", l, b)
            put("dve", t + 0.4, "rstd2", l, b)
        advance(1.0)

    def ln_tile(l, b, kind, slot, tt):
        g = take("g")
        not_before(("g", g - 2))
        put("dve", state["t"] - 0.5, "xn", l, b, kind, tt, g)
        put("pe", state["t"], "xtr", g, l, b, kind, tt)
        e = advance(0.9)
        put("act", e + 0.1, "xhi", g, kind, slot, tt)
        due_at["g", g] = due_at["x", slot] = put("dve", e + 0.6, "xlo", g, kind, slot, tt)

    def ctx_tile(slot, kt):
        g = take("g")
        not_before(("g", g - 2), "norm")
        put("pe", state["t"], "ctr", g, kt)
        e = advance(0.9)
        put("act", e + 0.1, "chi", g, slot, kt)
        due_at["g", g] = due_at["x", slot] = put("dve", e + 0.6, "clo", g, slot, kt)

    def qk_job(kind, l, b, m, xslot, octet):
        g, n = take("g"), take("qk")
        not_before(("g", g - 2), ("x", xslot))
        c = chunk((kind, l, m), 2.6)
        put("pe", state["t"], "proj", c, g, xslot, P)
        e = advance(2.6)
        put("act", e + 0.1, "qhi", n, g, kind, l, m)
        due_at["g", g] = put("dve", e + 0.6, "qres", n, g, kind, l, m)
        put("act", e + 1.2, "qmid", n)
        put("pool", e + 1.8, "qlo", n)
        put("sp", e + 2.5, "qkout", n)
        due_at[kind, octet] = put("sp", e + 4.5, "qkin", n, kind, l, b, octet)

    def v_job(l, b, xslot, part):
        a = take("acc")
        not_before(("acc", a - 2), ("acc", a - 1), ("x", xslot))
        if l == 0:
            c = chunk(("v", 0, 0), 2.6)
            put("pe", state["t"], "v0", c, a, xslot)
            accs = (a,)
            e = advance(2.6)
        else:
            a2 = take("acc")
            accs = (a, a2)
            for i in range(2):
                c = chunk(("v", 1, part * 2 + i), 2.6)
                put("pe", state["t"], "v1", c, a, xslot, i)
                e = advance(2.6)
        for i, x in enumerate(accs):
            due_at["acc", x] = put("dve", e + 0.1 + 2.5 * i, "vsum", x, l, b, part, i)
            put("act", e + 0.7 + 2.5 * i, "vhi", x, l, b, part, i)
            put("pool", e + 1.2 + 2.5 * i, "vres", x, l, b, part, i)
            put("act", e + 1.8 + 2.5 * i, "vmid", x, l, b, part, i)
            due_at["v", l, b] = put("pool", e + 2.4 + 2.5 * i, "vlo", x, l, b, part, i)

    def ffn_job(l, xslot, f, which):
        m = min(P, FF[l] - f * P)
        g = take("g")
        not_before(("g", g - 2), ("x", xslot))
        c = chunk((which, l, f), 2.6)
        put("pe", state["t"], "proj", c, g, xslot, m)
        e = advance(2.6)
        if which == "g":
            n = take("gate")
            k = max(e + 0.1, due_at.get(("gate", n - 2), -1e9) + 0.01)
            put("act", k, "tanh", n, g, m)
            due_at["g", g] = put("dve", k + 0.6, "gsum", n, g, m)
        else:
            n = state["gate"] - 1
            due_at["g", g] = due_at["gate", n] = put("dve", e + 0.7, "hmul", n, g, f, m)

    def out_chunk(l, b, slot, nh, kind, c, first, last):
        n = 2 if kind == "o" else min(2, FT[l] - 2 * c)
        if first:
            state["a"] = take("acc")
            take("acc")
            not_before(("acc", state["a"] - 2), ("acc", state["a"] - 1), ("x", slot))
        rows, hs = [], []
        for i in range(n):
            rows.append(P if kind == "o" else min(P, FF[l] - (2 * c + i) * P))
        w = chunk(("o" if kind == "o" else "d", l, nh, c), 1.3 * n)
        for i in range(n):
            if kind == "d":
                h = take("hs")
                k = max(state["t"] + 1.3 * i - 3.0, hs_end[h - HSPLIT] + 0.01 if h >= HSPLIT else -1e9)
                put("act", k, "hhi", h, 2 * c + i, rows[i])
                put("dve", k + 0.6, "hlo", h, 2 * c + i, rows[i])
                hs_end.append(state["t"] + 1.3 * (i + 1))
                due_at["hs", h] = k + 0.6
                hs.append(h)
        for i in range(n):
            if hs:
                not_before(("hs", hs[i]))
            put("pe", state["t"], "out", w, state["a"], slot, 2 * c + i if kind == "o" else -1,
                hs[i] if hs else -1, i, rows[i], first and i == 0, last and i == n - 1, i == n - 1)
            e = advance(1.3)
        if last:
            for i in range(2):
                due_at["acc", state["a"] + i] = put("dve", e + 0.1 + 1.0 * i, "xadd", state["a"] + i, l, b, nh, i)
                due_at["xbias", l, b] = put("pool", e + 0.7 + 1.0 * i, "xbias", state["a"] + i, l, b, nh, i)
                if l == 1:
                    put("sp", e + 1.6 + 1.0 * i, "store", state["a"] + i, b, nh, i)

    def score(u, i):
        r = take("ring")
        not_before(("ring", r - SRING), ("q", u // 4), ("k", u // 4 if u >= 2 * PAIRS else u // 16 * 4))
        put("pe", state["t"], "S", r, u, i)
        due_at["ring", r] = put("dve", advance(0.22) + 0.3, "smax", r, u, i)

    def msplit(u, key):
        due_at["msplit", u] = put("dve", key, "msplit", u)

    def mtrans(u):
        r = take("ring")
        not_before(("ring", r - SRING), ("msplit", u))
        put("pe", state["t"], "Mt", r, u)
        e = advance(0.1)
        due_at["ring", r] = put("dve", e + 0.3, "mrow", r, u)
        put("sp", e + 0.9, "mout", u)
        due_at["min", u] = put("sp", e + 3.2, "min", u)

    def trans(u, i):
        r, j = take("ring"), take("tj")
        not_before(("ring", r - SRING), ("min", u))
        put("pe", state["t"], "T", r, j, u, i)
        e = max(advance(0.22) + 0.2, due_at.get(("plo", j - 2), -1e9) + 0.01)
        due_at["ring", r] = put("act", e, "exp", r, j, i)
        put("pool", e + 0.6, "mask", j, i)
        put("act", e + 1.2, "phi", j)
        due_at["plo", j] = put("dve", e + 1.8, "plo", j)

    def pv(u, half):
        not_before("norm", ("plo", 5 * u + 4), ("v",) + PHASES[u // PAIRS], ("v", 0, 1) if u < PAIRS else "")
        put("pe", state["t"], "PV", u, half)
        e = advance(0.55)
        if half == 1:
            due_at["norm"] = put("dve", e + 0.2, "norm", u)

    def attention_steps(p):
        steps, last = [], 4 * 16
        if p + 1 < last and p >= -1:
            steps.append((0.1, lambda: mtrans(p + 1)))
        if 0 <= p + 2 < last:
            s = [(0.22, lambda i=i: score(p + 2, i)) for i in range(5)]
        else:
            s = []
        v = [(0.55, lambda i=i: pv(p - 1, i)) for i in range(2)] if 1 <= p <= last else []
        t = [(0.22, lambda i=i: trans(p, i)) for i in range(5)] if 0 <= p < last else []
        order = s[:1] + t[:1] + s[1:3] + v + steps
        for i in range(4):
            order += t[i + 1:i + 2] + s[i + 3:i + 4]
        if 0 <= p + 2 < last:
            order.append((0.0, lambda: msplit(p + 2, state["t"] + 0.9)))
        return order

    def weave(attn, fill):
        total = sum(c for c, _ in fill)
        done, k = 0.0, 0
        for c, run in fill:
            while k < len(attn) and total and k / len(attn) <= done / total:
                attn[k][1]()
                k += 1
            run()
            done += c
        for _, run in attn[k:]:
            run()

    def w_ln(l, b, kind, slot, stats):
        w = [(0.1, lambda: ln_stats(l, b))] if stats else []
        return w + [(0.9, lambda tt=tt: ln_tile(l, b, kind, slot, tt)) for tt in range(TT)]

    def w_v(l, b, xslot):
        return [(2.6 if l == 0 else 5.2, lambda part=part: v_job(l, b, xslot, part)) for part in range(1 + l)]

    def w_qk(ph, o, xslot):
        l, b = PHASES[ph]
        w = [(2.6, lambda: qk_job("q", l, b, o, xslot, 4 * ph + o))]
        if l == 1:
            w.append((2.6, lambda: qk_job("k", l, b, o, xslot, 4 * ph + o)))
        return w

    def w_ffn(l, xslot):
        return [(2.6, lambda f=f, w=w: ffn_job(l, xslot, f, w)) for f in range(FT[l]) for w in "gu"]

    def w_out(l, b, slot):
        w = []
        for nh in range(2):
            parts = [("o", c) for c in range(2)] + [("d", c) for c in range(-(-FT[l] // 2))]
            for i, (k, c) in enumerate(parts):
                n = 2 if k == "o" else min(2, FT[l] - 2 * c)
                w.append((1.3 * n, lambda i=i, k=k, c=c, nh=nh: out_chunk(
                    l, b, slot, nh, k, c, i == 0, i == len(parts) - 1)))
        return w

    for _, run in w_ln(0, 0, "x", 0, True) + w_qk(0, 0, 0):
        run()
    qk_job("k", 0, 0, 0, 0, 0)
    for _, run in w_v(0, 0, 0) + w_ln(0, 1, "x", 1, True):
        run()
    qk_job("k", 0, 1, 0, 1, 0)
    for _, run in w_v(0, 1, 1):
        run()
    weave([], w_ln(0, 0, "n", 1, False))
    advance(3.0)
    for p in (-2, -1):
        weave(attention_steps(p), w_ffn(0, 1)[8 * (p + 2):8 * (p + 2) + 8])
    ffn00 = w_ffn(0, 1)[16:]

    free = [
        ffn00,
        w_out(0, 0, 1) + w_ln(0, 1, "n", 1, False) + w_ffn(0, 1),
        w_out(0, 1, 1) + w_ffn(1, 0),
        w_out(1, 0, 0) + w_ffn(1, 1),
    ]
    due = [
        {10: w_ln(0, 1, "x", 0, False)},
        {10: w_ln(1, 0, "x", 0, True) + w_v(1, 0, 0)},
        {9: [(0.0, lambda: put("sp", state["t"], "bo1"))], 10: w_ln(1, 1, "x", 1, True) + w_v(1, 1, 1)},
        {},
    ]
    xslot_of = (0, 0, 0, 1)
    for ph in range(4):
        for o in range(4):
            nxt = (ph, o + 1) if o < 3 else (ph + 1, 0)
            if nxt[0] < 4:
                due[ph].setdefault(4 * o, [])
                due[ph][4 * o] = due[ph][4 * o] + w_qk(nxt[0], nxt[1], xslot_of[nxt[0]])
        total = sum(c for c, _ in free[ph]) + sum(c for w in due[ph].values() for c, _ in w)
        spent, queue = 0.0, list(free[ph])
        for s in range(SLOTS):
            pinned, more = list(due[ph].get(s, [])), []
            spent += sum(c for c, _ in pinned)
            first = 1 if ph and s == 0 else 0
            if not first:
                while queue and (spent < total * (s + 1) / SLOTS or s == SLOTS - 1):
                    more.append(queue.pop(0))
                    spent += more[-1][0]
            fill = []
            while pinned or more:
                fill += [pinned.pop(0)] if pinned else []
                fill += [more.pop(0)] if more else []
            weave(attention_steps(16 * ph + s), fill)
            if first:
                for kt in range(KT):
                    ctx_tile((1, 1, 0)[ph - 1], kt)
    weave(attention_steps(64), [])
    for kt in range(KT):
        ctx_tile(0, kt)
    for _, run in w_out(1, 1, 0):
        run()
    return {e: [s for _, _, s in sorted(x, key=lambda x: x[:2])] for e, x in line.items()}


def numbered(steps, *kinds):
    out = {}
    for s in steps:
        if s[0] in kinds:
            out[s] = len(out) + 1
    return out


def by(numbers, *at):
    return {tuple(s[i] for i in at) if len(at) > 1 else s[at[0]]: n for s, n in numbers.items()}


def two_layers(nc, x_in, weights, qk_bias, ln_w, bv, bo0, bo1, qk_scratch, m_scratch, out):
    steps = plan()
    PE, SE, VE, GP, SP = (steps[e] for e in ("pe", "act", "dve", "pool", "sp"))

    n_split = by(numbered(GP, "wlo"), 1)
    n_whi = by(numbered(SE, "whi"), 1)
    n_g_made, n_acc_made, n_chunk_used, n_out_used, count = {}, {}, {}, {}, 0
    for s in PE:
        if s[0] in ("xtr", "ctr"):
            count += 1
            n_g_made[s[1]] = count
        elif s[0] == "proj":
            count += 1
            n_g_made[s[2]] = n_chunk_used[s[1]] = count
        elif s[0] == "v0":
            count += 1
            n_acc_made[s[2]] = n_chunk_used[s[1]] = count
        elif s[0] in ("v1", "out"):
            if s[4] == 1 if s[0] == "v1" else s[9]:
                count += 1
                n_acc_made[s[2]] = count
                n_acc_made[s[2] + 1] = count + 1
            count += 1
            n_chunk_used[s[1]] = count
            if s[0] == "out" and s[5] >= 0:
                n_out_used[s[5]] = count
    g_free = numbered(VE, "qres", "gsum", "hmul", "xlo", "clo")
    n_g_free = {s[1] if s[0] in ("xlo", "clo") else s[2]: n for s, n in g_free.items()}
    n_acc_free = by(numbered(VE, "vsum", "xadd"), 1)
    ring_step = {s[1]: s for s in PE if s[0] in ("S", "T", "Mt")}
    n_ring = by(numbered(PE, "S", "T", "Mt"), 1)
    n_smax = by(numbered(VE, "smax", "mrow"), 1)
    n_exp = by(numbered(SE, "exp"), 2)
    exp_of_ring = {s[1]: n_exp[s[2]] for s in SE if s[0] == "exp"}
    last_smax = {s[2]: n_smax[s[1]] for s in VE if s[0] == "smax" and s[3] == 4}
    mrow_of = {s[2]: n_smax[s[1]] for s in VE if s[0] == "mrow"}
    t_of = {(s[3], s[4]): n_ring[s[1]] for s in PE if s[0] == "T"}
    mt_of = {s[2]: n_ring[s[1]] for s in PE if s[0] == "Mt"}
    n_mask = by(numbered(GP, "mask"), 1)
    n_phi = by(numbered(SE, "phi"), 1)
    n_plo = by(numbered(VE, "plo"), 1)
    n_pv = {s[1]: i + 1 for i, s in enumerate(s for s in PE if s[0] == "PV" and s[2] == 1)}
    n_norm = by(numbered(VE, "norm"), 1)
    n_msplit = by(numbered(VE, "msplit"), 1)
    n_qhi = by(numbered(SE, "qhi"), 1)
    n_qmid = by(numbered(SE, "qmid"), 1)
    n_qlo = by(numbered(GP, "qlo"), 1)
    n_vhi = by(numbered(SE, "vhi"), 1)
    n_vmid = by(numbered(SE, "vmid"), 1)
    n_vlo = by(numbered(GP, "vlo"), 1)
    n_vres = by(numbered(GP, "vres"), 1)
    n_xbias = by(numbered(GP, "xbias"), 1)
    n_xbias_l0 = max(n_xbias[s[1]] for s in GP if s[0] == "xbias" and s[2] == 0)
    n_tanh = by(numbered(SE, "tanh"), 1)
    n_xhi = by(numbered(SE, "xhi", "chi"), 1)
    n_hhi = by(numbered(SE, "hhi"), 1)
    n_hlo = by(numbered(VE, "hlo"), 1)
    n_xn = by(numbered(VE, "xn"), 5)
    n_stats = by(numbered(VE, "stats", "rstd", "rstd2"), 0, 1, 2)
    n_root = by(numbered(SE, "root", "root2"), 0, 1, 2)
    arrival, qk_read, seen = {}, {}, {}
    for s in SP:
        if s[0] == "qkin":
            _, n, what, l, b, octet = s
            slots = (0, 1) if what == "k" and l == 0 else (octet % 2,)
            qk_read[n] = []
            for slot in slots:
                seen[(what, slot)] = seen.get((what, slot), 0) + 6 * 16
                arrival[(what, octet)] = seen[(what, slot)]
                qk_read[n].append((what, slot, seen[(what, slot)]))
            if len(slots) == 2:
                for o in range(8):
                    arrival[("k", o)] = seen[("k", 0)]
    vlo_at = {(s[2], s[3]): n_vlo[s[1]] for s in GP if s[0] == "vlo"}

    with ExitStack() as ctx:
        def sb(name, shape, dt):
            return ctx.enter_context(nc.sbuf_tensor(name, shape, dt))

        def sem(name):
            return ctx.enter_context(nc.semaphore(name))

        x = sb("x", [P, B * TT, D], F32)
        xt_hi = sb("xt_hi", [P, 2, KT, T], F32R)
        xt_lo = sb("xt_lo", [P, 2, KT, T], F32R)
        h = sb("h", [P, FT[0], T], F32)
        h_hi = sb("h_hi", [P, HSPLIT, T], F32R)
        h_lo = sb("h_lo", [P, HSPLIT, T], F32R)
        w_raw = sb("w_raw", [P, RAW, 512], F32)
        w_hi = sb("w_hi", [P, SPLIT, 512], F32R)
        w_lo = sb("w_lo", [P, SPLIT, 512], F32R)
        q_op = sb("q_op", [MROWS, 2, 8, T], BF16)
        k_op = sb("k_op", [MROWS, 2, 8, T], BF16)
        v_op = sb("v_op", [P, 2, TT, H, VW], BF16)
        context = sb("context", [P, TT, D], F32)
        p32 = sb("p32", [P, 2, 512], F32)
        p_hi = sb("p_hi", [P, PRING, 512], F16)
        p_lo = sb("p_lo", [P, PRING, 512], F16)
        qk_parts = sb("qk_parts", [P, 2, 3, T], BF16)
        rest = sb("rest", [P, 512], F32)
        xn = sb("xn", [P, D], F32)
        gate = sb("gate", [P, 2, T], F32)
        causal = sb("causal", [P, 512], BF16)
        ident = sb("ident", [P, P], F32)
        ident16 = sb("ident16", [P, P], BF16)
        bv_all = sb("bv_all", [P, D], F32)
        bo_all = sb("bo_all", [P, D], F32)
        biases = sb("biases", [P, 2, 2, 4], F32)
        lnw = sb("lnw", [P, KT], F32)
        maxima = sb("maxima", [P, 2, 8], F32)
        m_rest = sb("m_rest", [P, 8], F32)
        m_parts = sb("m_parts", [P, 2, 3, 8], BF16)
        m_rows = sb("m_rows", [24, 2, P], BF16)
        pv_sum = sb("pv_sum", [P, TT, 2, HD], F32)
        recip = sb("recip", [P, TT, 2], F32)
        bn = sb("bn", [P, TT, 6], F32)
        mv = sb("mv", [P, B, TT, 2], F32)
        ve = sb("ve", [P, TT], F32)
        ms = sb("ms", [P, TT], F32)
        root = sb("root", [P, TT], F32)
        root2 = sb("root2", [P, TT], F32)
        newton = sb("newton", [P, TT], F32)
        rstd = sb("rstd", [P, B, TT], F32)
        rstd_n = sb("rstd_n", [P, B, TT], F32)

        s_ring = [ctx.enter_context(nc.psum_tensor(f"s_ring{i}", [P, 512], F32)) for i in range(SRING)]
        g_ring = [ctx.enter_context(nc.psum_tensor(f"g_ring{i}", [P, 512], F32)) for i in range(2)]
        acc = [ctx.enter_context(nc.psum_tensor(f"acc{i}", [P, 512], F32)) for i in range(2)]
        pv_ps = ctx.enter_context(nc.psum_tensor("pv_ps", [P, 512], F32))

        raw_here = [sem(f"raw_here{i}") for i in range(RAW)]
        x_here = [sem(f"x_here{i}") for i in range(B)]
        consts_here = sem("consts_here")
        bo_here = sem("bo_here")
        consts_made = sem("consts_made")
        ones_made = sem("ones_made")
        whi_done, split_done, work_done = sem("whi_done"), sem("split_done"), sem("work_done")
        g_freed, acc_freed = sem("g_freed"), sem("acc_freed")
        ring_made, smax_done, exp_done = sem("ring_made"), sem("smax_done"), sem("exp_done")
        mask_done, phi_done, plo_done = sem("mask_done"), sem("phi_done"), sem("plo_done")
        pv_done, norm_done, msplit_done = sem("pv_done"), sem("norm_done"), sem("msplit_done")
        qhi_done, qmid_done, qlo_done = sem("qhi_done"), sem("qmid_done"), sem("qlo_done")
        vhi_done, vmid_done, vlo_done = sem("vhi_done"), sem("vmid_done"), sem("vlo_done")
        vres_done = sem("vres_done")
        tanh_done, xhi_done = sem("tanh_done"), sem("xhi_done")
        hhi_done, hlo_done = sem("hhi_done"), sem("hlo_done")
        xn_done, stats_done, root_done = sem("xn_done"), sem("stats_done"), sem("root_done")
        dve_chain, pool_chain = sem("dve_chain"), sem("pool_chain")
        qk_out = [sem(f"qk_out{i}") for i in range(2)]
        q_here = [sem(f"q_here{i}") for i in range(2)]
        k_here = [sem(f"k_here{i}") for i in range(2)]
        m_out = [sem(f"m_out{i}") for i in range(2)]
        m_here = [sem(f"m_here{i}") for i in range(2)]
        xbias_done = sem("xbias_done")
        stored = sem("stored")
        block = ctx.enter_context(nc.Block())

        hmul_of_gate = {s[1]: g_free[s] for s in VE if s[0] == "hmul"}
        gsum_of_gate = {s[1]: g_free[s] for s in VE if s[0] == "gsum"}
        qk_g = {s[1]: s[2] for s in SE if s[0] == "qhi"}
        xtr_made = {n_xn[s[1]]: n_g_made[s[1]] for s in PE if s[0] == "xtr"}
        x_final = {}
        for s in VE:
            if s[0] == "xadd":
                x_final[(s[2], s[3])] = max(n_xbias[s[1]], x_final.get((s[2], s[3]), 0))
        ctrs = [s for s in PE if s[0] == "ctr"]
        ctx_used = {i: n_g_made[ctrs[4 * i + 3][1]] for i in range(4)}
        v_before = {(0, 0): None, (0, 1): None, (1, 0): None, (1, 1): n_pv[2 * PAIRS - 1]}
        rest_before, before = {}, None
        for s in VE:
            if s[0] in ("qres", "vsum"):
                rest_before[s] = before
                before = (qlo_done, n_qlo[s[1]]) if s[0] == "qres" else (vlo_done, n_vlo[s[1]])
        splits = [s for s in VE if s[0] == "hlo"]
        tiles = [s for s in VE if s[0] == "hmul"]
        f_before, last_hmul = {}, {}
        per_phase = [2 * FT[l] for l, _ in PHASES]
        for ph in range(4):
            mine = tiles[sum(FT[l] for l, _ in PHASES[:ph]):][:FT[PHASES[ph][0]]]
            for s in mine:
                f_before[s] = (hlo_done, sum(per_phase[:ph])) if ph else None
            for s in splits[sum(per_phase[:ph]):][:per_phase[ph]]:
                last_hmul[s[1]] = g_free[mine[-1]]

        def h_written(hs):
            return last_hmul[hs]

        reads = {0: None, 1: None}
        x_last_read = {}
        x_free_count = {}
        writes = {0: 0, 1: 0}
        slot_of_g = {s[1]: s[3] if s[0] == "xhi" else s[2] for s in SE if s[0] in ("xhi", "chi")}
        for s in PE:
            if s[0] in ("xtr", "ctr"):
                g = s[1]
                slot = slot_of_g[g]
                x_last_read[g] = reads[slot]
                writes[slot] = n_g_free[g]
            elif s[0] == "proj":
                reads[s[3]] = n_g_made[s[2]]
                x_free_count[s] = writes[s[3]]
            elif s[0] in ("v0", "v1"):
                reads[s[3]] = n_chunk_used[s[1]]
                x_free_count[s] = writes[s[3]]
            elif s[0] == "out" and s[4] >= 0:
                reads[s[3]] = n_chunk_used[s[1]]
                x_free_count[s] = writes[s[3]]

        def k_slot_and_head(u, j):
            head = 2 * (u % PAIRS) + j
            if u < 2 * PAIRS:
                return u // PAIRS, head // REP
            return u // 4 % 2, head % 8

        def v_head(u, j):
            l, b = PHASES[u // PAIRS]
            head = 2 * (u % PAIRS) + j
            if l == 1:
                return b, head
            from_batch, group = head // REP % 2, b * (G // 2) + head // (2 * REP)
            return 1, G * from_batch + group

        def v_view(l, b, part, i, piece):
            if l == 0:
                return v_op[:, 1, :, G * b:G * b + G, piece * HD:(piece + 1) * HD]
            heads = slice(part * 16, part * 16 + 16)
            return v_op[:, b, 2 * i:2 * i + 2, heads, piece * HD:(piece + 1) * HD]

        def v_like(flat, l):
            return flat.rearrange("p (t h d) -> p t h d", t=TT if l == 0 else 2, d=HD)

        @block.sync
        def _(sp):
            for b in range(B):
                sp.dma_start(x[:, b * TT:(b + 1) * TT, :],
                             x_in[b].rearrange("(t p) d -> p t d", p=P)).then_inc(x_here[b], 16)
                if b == 0:
                    sp.dma_start(biases[:, :, :, :], qk_bias).then_inc(consts_here, 16)
                    sp.dma_start(lnw[:, :], ln_w).then_inc(consts_here, 16)
            sp.dma_start(bv_all[:, :], bv.unsqueeze(0).to_broadcast([P, D])).then_inc(consts_here, 16)
            sp.dma_start(bo_all[:, :], bo0.unsqueeze(0).to_broadcast([P, D])).then_inc(bo_here, 16)
            stores = 0
            for s in SP:
                kind = s[0]
                if kind == "qkout":
                    n = s[1]
                    sp.wait_ge(qlo_done, n_qlo[n])
                    if n >= 2:
                        for what, slot, count in qk_read[n - 2]:
                            sp.wait_ge((q_here if what == "q" else k_here)[slot], count)
                    sp.dma_start(qk_scratch[n % 2], qk_parts[:, n % 2, :, :]).then_inc(qk_out[n % 2], 16)
                elif kind == "qkin":
                    _, n, what, l, b, octet = s
                    sp.wait_ge(qk_out[n % 2], 16 * (n // 2 + 1))
                    dst, parts, here = (q_op, Q_PARTS, q_here) if what == "q" else (k_op, K_PARTS, k_here)
                    if what == "q" and octet >= 2:
                        sp.wait_ge(ring_made, t_of[(4 * (octet - 2) + 3, 4)])
                    if what == "k" and l == 1:
                        last = 15 if octet == 8 else 31 if octet == 9 else 4 * (octet - 2) + 3
                        sp.wait_ge(ring_made, t_of[(last, 4)])
                    rows = qk_scratch[n % 2].rearrange("(h d) s t -> d h s t", d=HD)
                    for g, part in enumerate(parts):
                        to = dst[g * HD:(g + 1) * HD]
                        if what == "k" and l == 0:
                            for slot in range(2):
                                sp.dma_start(to[:, slot, b:8:2, :], rows[:, 4 * slot:4 * slot + 4, part, :]
                                             ).then_inc(here[slot], 16)
                        else:
                            sp.dma_start(to[:, octet % 2, :, :], rows[:, :, part, :]
                                         ).then_inc(here[octet % 2], 16)
                elif kind == "mout":
                    u = s[1]
                    sp.wait_ge(smax_done, mrow_of[u])
                    if u >= 2:
                        sp.wait_ge(m_here[u % 2], 16 * (u // 2))
                    sp.dma_start(m_scratch[u % 2], m_rows[:, u % 2, :]).then_inc(m_out[u % 2], 16)
                elif kind == "min":
                    u = s[1]
                    sp.wait_ge(m_out[u % 2], 16 * (u // 2 + 1))
                    if u >= 8:
                        sp.wait_ge(ring_made, t_of[(u - 8, 4)])
                    h0 = 2 * (u % 4)
                    sp.dma_start(q_op[QROWS:MROWS, u // 4 % 2, h0:h0 + 2, :].rearrange("c h t -> c (h t)"),
                                 m_scratch[u % 2].rearrange("(c r) t -> c (r t)", c=3)
                                 ).then_inc(m_here[u % 2], 16)
                elif kind == "bo1":
                    sp.wait_ge(xbias_done, n_xbias_l0)
                    sp.dma_start(bo_all[:, :], bo1.unsqueeze(0).to_broadcast([P, D])).then_inc(bo_here, 16)
                elif kind == "store":
                    _, a, b, nh, i = s
                    sp.wait_ge(xbias_done, n_xbias[a])
                    sp.dma_start(out[b].rearrange("(t p) d -> p t d", p=P)
                                 [:, 2 * i:2 * i + 2, nh * HALF:(nh + 1) * HALF],
                                 x[:, b * TT + 2 * i:b * TT + 2 * i + 2, nh * HALF:(nh + 1) * HALF]
                                 ).then_inc(stored, 16)
                    stores += 1
            sp.wait_ge(stored, 16 * stores)

        @block.gpsimd
        def _(pool):
            chain = [0]

            def link(ins):
                chain[0] += 1
                ins.then_inc(pool_chain, 1)
                pool.wait_ge(pool_chain, chain[0])

            link(pool.memset(ident[:, :], 0.0))
            pool.affine_select(out=ident[:, :], in_=ident[:, :], compare_op=ALU.not_equal, fill=1.0,
                               base=0, pattern=[[-1, P]], channel_multiplier=1).then_inc(consts_made, 1)
            link(pool.memset(ident16[:, :], 0.0))
            pool.affine_select(out=ident16[:, :], in_=ident16[:, :], compare_op=ALU.not_equal, fill=1.0,
                               base=0, pattern=[[-1, P]], channel_multiplier=1).then_inc(consts_made, 1)
            link(pool.memset(causal[:, :], 0.0))
            pool.affine_select(out=causal[:, 512 - P:], in_=causal[:, 512 - P:], compare_op=ALU.is_ge,
                               fill=LOWEST, base=0, pattern=[[-1, P]], channel_multiplier=1
                               ).then_inc(consts_made, 1)
            pool.wait_ge(consts_made, 3)
            link(pool.memset(k_op[QROWS:MROWS, :, :, :], 1.0))
            pool.memset(v_op[:, :, :, :, 3 * HD:3 * HD + 1].rearrange("p s t h c -> p (s t h) c"), 1.0
                        ).then_inc(ones_made, 1)
            for s in GP:
                kind = s[0]
                if kind == "wlo":
                    c = s[1]
                    pool.wait_ge(whi_done, n_whi[c])
                    pool.tensor_tensor(w_lo[:, c % SPLIT, :], w_raw[:, c % RAW, :],
                                       w_hi[:, c % SPLIT, :].bitcast(F32), ALU.subtract
                                       ).then_inc(split_done, 1)
                elif kind == "qlo":
                    n = s[1]
                    pool.wait_ge(qmid_done, n_qmid[n])
                    pool.tensor_tensor(qk_parts[:, n % 2, 2, :], rest[:, :], qk_parts[:, n % 2, 1, :],
                                      ALU.subtract).then_inc(qlo_done, 1)
                elif kind == "vres":
                    _, a, l, b, part, i = s
                    pool.wait_ge(vhi_done, n_vhi[a])
                    pool.tensor_tensor(v_like(rest[:, :], l), v_like(rest[:, :], l),
                                      v_view(l, b, part, i, 0), ALU.subtract).then_inc(vres_done, 1)
                elif kind == "vlo":
                    _, a, l, b, part, i = s
                    pool.wait_ge(vmid_done, n_vmid[a])
                    pool.tensor_tensor(v_view(l, b, part, i, 2), v_like(rest[:, :], l),
                                      v_view(l, b, part, i, 1), ALU.subtract).then_inc(vlo_done, 1)
                elif kind == "xbias":
                    _, a, l, b, nh, i = s
                    pool.wait_ge(acc_freed, n_acc_free[a])
                    pool.wait_ge(bo_here, 16 * (l + 1))
                    at = slice(b * TT + 2 * i, b * TT + 2 * i + 2)
                    dst = x[:, at, nh * HALF:(nh + 1) * HALF]
                    bias = bo_all[:, nh * HALF:(nh + 1) * HALF].unsqueeze(1).to_broadcast([P, 2, HALF])
                    pool.tensor_tensor(dst, dst, bias, ALU.add).then_inc(xbias_done, 1)
                else:
                    _, j, i = s
                    pool.wait_ge(exp_done, n_exp[j])
                    view = p32[:, j % 2, :]
                    if i in (0, 2):
                        view, n = view[:, 0:P], 1
                    elif i in (1, 3):
                        view, n = view.rearrange("p (b t) -> p b t", b=4)[:, 0:4:3, :], 2
                    else:
                        view, n = view.rearrange("p (b t) -> p b t", b=4)[:, 0:4:2, :], 2
                    pool.affine_select(out=view, in_=view, compare_op=ALU.is_ge, fill=0.0, base=0,
                                       pattern=[[0, n], [1, P]] if n == 2 else [[1, P]],
                                       channel_multiplier=-1).then_inc(mask_done, 1)

        @block.scalar
        def _(act):
            act.wait_ge(consts_made, 3)
            act.wait_ge(consts_here, 48)
            for s in SE:
                kind = s[0]
                if kind == "wload":
                    _, c, at = s
                    if c >= RAW:
                        act.wait_ge(split_done, n_split[c - RAW])
                    act.dma_start(w_raw[:, c % RAW, :], weights[at]).then_inc(raw_here[c % RAW], 16)
                elif kind == "exp":
                    _, r, j, i = s
                    act.wait_ge(ring_made, n_ring[r])
                    if j >= 2:
                        act.wait_ge(plo_done, n_plo[j - 2])
                    act.activation(p32[:, j % 2, :], s_ring[r % SRING][:, :], ACT.Exp, scale=SCALE
                                   ).then_inc(exp_done, 1)
                elif kind == "whi":
                    c = s[1]
                    act.wait_ge(raw_here[c % RAW], 16 * (c // RAW + 1))
                    if c >= SPLIT:
                        act.wait_ge(work_done, n_chunk_used[c - SPLIT])
                    act.activation(w_hi[:, c % SPLIT, :], w_raw[:, c % RAW, :], ACT.Copy).then_inc(whi_done, 1)
                elif kind == "phi":
                    j = s[1]
                    act.wait_ge(mask_done, n_mask[j])
                    if j >= PRING:
                        act.wait_ge(pv_done, n_pv[(j - PRING) // 5])
                    act.activation(p_hi[:, j % PRING, :], p32[:, j % 2, :], ACT.Copy).then_inc(phi_done, 1)
                elif kind == "tanh":
                    _, n, g, m = s
                    act.wait_ge(work_done, n_g_made[g])
                    if n >= 2:
                        act.wait_ge(g_freed, hmul_of_gate[n - 2])
                    act.activation(gate[0:m, n % 2, :], g_ring[g % 2][0:m, :], ACT.Tanh, scale=0.5
                                   ).then_inc(tanh_done, 1)
                elif kind in ("xhi", "chi"):
                    g = s[1]
                    act.wait_ge(work_done, n_g_made[g])
                    if x_last_read[g] is not None:
                        act.wait_ge(work_done, x_last_read[g])
                    ps = g_ring[g % 2][:, :].rearrange("p (k t) -> p k t", k=KT)
                    if kind == "chi":
                        act.activation(xt_hi[:, s[2], s[3], :], g_ring[g % 2][:, :], ACT.Copy
                                       ).then_inc(xhi_done, 1)
                    else:
                        _, _, what, slot, tt = s
                        dst = xt_hi[:, slot, :, tt * P:(tt + 1) * P]
                        if what == "x":
                            act.activation(dst, ps, ACT.Copy).then_inc(xhi_done, 1)
                        else:
                            for kt in range(KT):
                                last = act.activation(dst[:, kt, :], ps[:, kt, :], ACT.Copy,
                                                      scale=lnw[:, kt:kt + 1])
                            last.then_inc(xhi_done, 1)
                elif kind == "qhi":
                    _, n, g, what, l, m = s
                    act.wait_ge(work_done, n_g_made[g])
                    if n >= 2:
                        act.wait_ge(qk_out[n % 2], 16 * (n // 2))
                    act.activation(qk_parts[:, n % 2, 0, :], g_ring[g % 2][:, :], ACT.Identity,
                                   bias=biases[:, l, "qk".index(what), m:m + 1]).then_inc(qhi_done, 1)
                elif kind == "qmid":
                    n = s[1]
                    act.wait_ge(g_freed, n_g_free[qk_g[n]])
                    act.activation(qk_parts[:, n % 2, 1, :], rest[:, :], ACT.Copy).then_inc(qmid_done, 1)
                elif kind == "vhi":
                    _, a, l, b, part, i = s
                    act.wait_ge(acc_freed, n_acc_free[a])
                    if v_before[(l, b)] is not None:
                        act.wait_ge(pv_done, v_before[(l, b)])
                    act.activation(v_view(l, b, part, i, 0), v_like(rest[:, :], l), ACT.Copy
                                   ).then_inc(vhi_done, 1)
                elif kind == "vmid":
                    _, a, l, b, part, i = s
                    act.wait_ge(vres_done, n_vres[a])
                    act.activation(v_view(l, b, part, i, 1), v_like(rest[:, :], l), ACT.Copy
                                   ).then_inc(vmid_done, 1)
                elif kind == "hhi":
                    _, hs, f, rows = s
                    act.wait_ge(g_freed, h_written(hs))
                    if hs >= HSPLIT:
                        act.wait_ge(work_done, n_out_used[hs - HSPLIT])
                    act.activation(h_hi[0:rows, hs % HSPLIT, :], h[0:rows, f, :], ACT.Copy
                                   ).then_inc(hhi_done, 1)
                elif kind == "root":
                    _, l, b = s
                    act.wait_ge(stats_done, n_stats[("stats", l, b)])
                    act.activation(root[:, :], ve[:, :], ACT.Sqrt).then_inc(root_done, 1)
                elif kind == "root2":
                    _, l, b = s
                    act.wait_ge(stats_done, n_stats[("rstd", l, b)])
                    act.activation(root2[:, :], ms[:, :], ACT.Sqrt).then_inc(root_done, 1)
                else:
                    raise AssertionError(kind)

        @block.vector
        def _(dve):
            chain = [0]

            def link(ins):
                chain[0] += 1
                ins.then_inc(dve_chain, 1)
                dve.wait_ge(dve_chain, chain[0])
                return chain[0]

            def inverse_root(dst, value, rooted):
                link(dve.reciprocal(dst, rooted))
                link(dve.tensor_tensor(newton[:, :], dst, dst, ALU.mult))
                link(dve.tensor_tensor(newton[:, :], newton[:, :], value, ALU.mult))
                link(dve.tensor_scalar(newton[:, :], newton[:, :], -0.5, 1.5, ALU.mult, ALU.add))
                return dve.tensor_tensor(dst, dst, newton[:, :], ALU.mult)

            dve.wait_ge(consts_made, 3)
            dve.wait_ge(consts_here, 48)
            for s in VE:
                kind = s[0]
                if kind == "stats":
                    _, l, b = s
                    if l == 0:
                        dve.wait_ge(x_here[b], 16)
                    else:
                        dve.wait_ge(xbias_done, x_final[(0, b)])
                    for tt in range(TT):
                        last = dve.bn_stats(bn[:, tt, :], x[:, b * TT + tt, :])
                    link(last)
                    for tt in range(TT):
                        last = dve.bn_aggr(mv[:, b, tt, :], bn[:, tt, :])
                    link(last)
                    dve.tensor_scalar(ve[:, :], mv[:, b, :, 1], EPS, None, ALU.add).then_inc(stats_done, 1)
                elif kind == "rstd":
                    _, l, b = s
                    dve.wait_ge(root_done, n_root[("root", l, b)])
                    if l == 1:
                        inverse_root(rstd[:, b, :], ve[:, :], root[:, :]).then_inc(stats_done, 1)
                    else:
                        link(inverse_root(rstd[:, b, :], ve[:, :], root[:, :]))
                        link(dve.tensor_tensor(ms[:, :], rstd[:, b, :], rstd[:, b, :], ALU.mult))
                        link(dve.tensor_tensor(ms[:, :], ms[:, :], mv[:, b, :, 1], ALU.mult))
                        dve.tensor_scalar(ms[:, :], ms[:, :], EPS, None, ALU.add).then_inc(stats_done, 1)
                elif kind == "rstd2":
                    _, l, b = s
                    dve.wait_ge(root_done, n_root[("root2", l, b)])
                    link(inverse_root(rstd_n[:, b, :], ms[:, :], root2[:, :]))
                    dve.tensor_tensor(rstd_n[:, b, :], rstd_n[:, b, :], rstd[:, b, :], ALU.mult
                                      ).then_inc(stats_done, 1)
                elif kind == "xn":
                    _, l, b, what, tt, g = s
                    n = n_xn[g]
                    dve.wait_ge(stats_done, n_stats[("rstd2" if l == 0 else "rstd", l, b)])
                    if n >= 2:
                        dve.wait_ge(work_done, xtr_made[n - 1])
                    scale = rstd if what == "x" else rstd_n
                    dve.tensor_scalar(xn[:, :], x[:, b * TT + tt, :], mv[:, b, tt, 0:1],
                                      scale[:, b, tt:tt + 1], ALU.subtract, ALU.mult).then_inc(xn_done, 1)
                elif kind in ("xlo", "clo"):
                    g = s[1]
                    dve.wait_ge(xhi_done, n_xhi[g])
                    ps = g_ring[g % 2][:, :].rearrange("p (k t) -> p k t", k=KT)
                    if kind == "clo":
                        dve.tensor_tensor(xt_lo[:, s[2], s[3], :], g_ring[g % 2][:, :],
                                          xt_hi[:, s[2], s[3], :].bitcast(F32), ALU.subtract
                                          ).then_inc(g_freed, 1)
                    else:
                        _, _, what, slot, tt = s
                        hi = xt_hi[:, slot, :, tt * P:(tt + 1) * P].bitcast(F32)
                        lo = xt_lo[:, slot, :, tt * P:(tt + 1) * P]
                        if what == "x":
                            dve.tensor_tensor(lo, ps, hi, ALU.subtract).then_inc(g_freed, 1)
                        else:
                            for kt in range(KT):
                                last = dve.scalar_tensor_tensor(
                                    out=lo[:, kt, :], in0=ps[:, kt, :], scalar=lnw[:, kt:kt + 1],
                                    in1=hi[:, kt, :], op0=ALU.mult, op1=ALU.subtract)
                            last.then_inc(g_freed, 1)
                elif kind == "qres":
                    _, n, g, what, l, m = s
                    dve.wait_ge(qhi_done, n_qhi[n])
                    if rest_before[s] is not None:
                        dve.wait_ge(*rest_before[s])
                    dve.scalar_tensor_tensor(
                        out=rest[:, :], in0=g_ring[g % 2][:, :],
                        scalar=biases[:, l, "qk".index(what), m:m + 1], in1=qk_parts[:, n % 2, 0, :],
                        op0=ALU.add, op1=ALU.subtract).then_inc(g_freed, 1)
                elif kind == "vsum":
                    _, a, l, b, part, i = s
                    dve.wait_ge(work_done, n_acc_made[a])
                    if rest_before[s] is not None:
                        dve.wait_ge(*rest_before[s])
                    if l == 0:
                        dve.tensor_copy(rest[:, :], acc[a % 2][:, :]).then_inc(acc_freed, 1)
                    else:
                        for t in range(2):
                            last = dve.tensor_tensor(
                                rest[:, t * HALF:(t + 1) * HALF], acc[a % 2][:, t * HALF:(t + 1) * HALF],
                                bv_all[:, part * HALF:(part + 1) * HALF], ALU.add)
                        last.then_inc(acc_freed, 1)
                elif kind == "gsum":
                    _, n, g, m = s
                    dve.wait_ge(tanh_done, n_tanh[n])
                    dve.scalar_tensor_tensor(
                        out=gate[0:m, n % 2, :], in0=gate[0:m, n % 2, :], scalar=1.0,
                        in1=g_ring[g % 2][0:m, :], op0=ALU.add, op1=ALU.mult).then_inc(g_freed, 1)
                elif kind == "hmul":
                    _, n, g, f, m = s
                    dve.wait_ge(g_freed, gsum_of_gate[n])
                    dve.wait_ge(work_done, n_g_made[g])
                    if f_before[s] is not None:
                        dve.wait_ge(*f_before[s])
                    dve.scalar_tensor_tensor(
                        out=h[0:m, f, :], in0=gate[0:m, n % 2, :], scalar=0.5,
                        in1=g_ring[g % 2][0:m, :], op0=ALU.mult, op1=ALU.mult).then_inc(g_freed, 1)
                elif kind == "hlo":
                    _, hs, f, rows = s
                    dve.wait_ge(hhi_done, n_hhi[hs])
                    dve.tensor_tensor(h_lo[0:rows, hs % HSPLIT, :], h[0:rows, f, :],
                                      h_hi[0:rows, hs % HSPLIT, :].bitcast(F32), ALU.subtract
                                      ).then_inc(hlo_done, 1)
                elif kind == "xadd":
                    _, a, l, b, nh, i = s
                    dve.wait_ge(work_done, n_acc_made[a])
                    at = slice(b * TT + 2 * i, b * TT + 2 * i + 2)
                    dst = x[:, at, nh * HALF:(nh + 1) * HALF]
                    dve.tensor_tensor(dst, acc[a % 2][:, :].rearrange("p (t n) -> p t n", t=2), dst,
                                      ALU.add).then_inc(acc_freed, 1)
                elif kind == "smax":
                    _, r, u, i = s
                    dve.wait_ge(ring_made, n_ring[r])
                    if i == 0 and u >= 2:
                        dve.wait_ge(msplit_done, n_msplit[u - 2])
                    if i in (0, 2):
                        parts = ((i // 2, 3, 0),)
                    elif i in (1, 3):
                        parts = ((i // 2, 2, 0), (i // 2, 0, 3 * P))
                    else:
                        parts = ((0, 1, 0), (1, 1, 2 * P))
                    for j, qt, at in parts:
                        n = (qt + 1) * P
                        last = dve.tensor_tensor_reduce(
                            out=s_ring[r % SRING][:, at:at + n], in0=s_ring[r % SRING][:, at:at + n],
                            in1=causal[:, 512 - n:], scale=1.0, scalar=LOWEST, op0=ALU.add, op1=ALU.max,
                            accum_out=maxima[:, u % 2, j * 4 + qt:j * 4 + qt + 1])
                    last.then_inc(smax_done, 1)
                elif kind == "msplit":
                    u = s[1]
                    dve.wait_ge(smax_done, last_smax[u])
                    if u >= 2:
                        dve.wait_ge(ring_made, mt_of[u - 2])
                    mp, mx = m_parts[:, u % 2, :, :], maxima[:, u % 2, :]
                    link(dve.tensor_scalar(mp[:, 0, :], mx, -1.0, None, ALU.mult))
                    link(dve.scalar_tensor_tensor(out=m_rest[:, :], in0=mx, scalar=-1.0, in1=mp[:, 0, :],
                                                  op0=ALU.mult, op1=ALU.subtract))
                    link(dve.tensor_copy(mp[:, 1, :], m_rest[:, :]))
                    dve.tensor_tensor(mp[:, 2, :], m_rest[:, :], mp[:, 1, :], ALU.subtract
                                      ).then_inc(msplit_done, 1)
                elif kind == "mrow":
                    _, r, u = s
                    dve.wait_ge(ring_made, n_ring[r])
                    if u >= 2:
                        dve.wait_ge(m_out[u % 2], 16 * (u // 2))
                    dve.tensor_copy(m_rows[:, u % 2, :], s_ring[r % SRING][:, :].bitcast(BF16)[0:24, 0:P]
                                    ).then_inc(smax_done, 1)
                elif kind == "plo":
                    j = s[1]
                    dve.wait_ge(phi_done, n_phi[j])
                    dve.tensor_tensor(p_lo[:, j % PRING, :], p32[:, j % 2, :], p_hi[:, j % PRING, :],
                                      ALU.subtract).then_inc(plo_done, 1)
                elif kind == "norm":
                    u = s[1]
                    dve.wait_ge(pv_done, n_pv[u])
                    if u % PAIRS == 0 and u:
                        dve.wait_ge(work_done, ctx_used[u // PAIRS - 1])
                    sums = pv_ps[:, 0:8 * VW].rearrange("p (g c) -> p g c", c=VW)
                    link(dve.reduce_sum(pv_sum[:, :, :, :].rearrange("p q j d -> p (q j) d"),
                                        sums[:, :, 0:3 * HD].rearrange("p g (s d) -> p g d s", s=3), AX))
                    link(dve.reciprocal(recip[:, :, :].rearrange("p q j -> p (q j)"), sums[:, :, 3 * HD]))
                    c0 = (u % PAIRS) * 2 * HD
                    dve.tensor_tensor(
                        context[:, :, c0:c0 + 2 * HD].rearrange("p q (j d) -> p q j d", j=2),
                        pv_sum[:, :, :, :], recip[:, :, :].unsqueeze(3).to_broadcast([P, TT, 2, HD]),
                        ALU.mult).then_inc(norm_done, 1)
                else:
                    raise AssertionError(kind)

        @block.tensor
        def _(pe):
            def three_passes(dst, w, xa, first, last, skip=False):
                for i, (a, c) in enumerate(((0, 0), (0, 1), (1, 0))):
                    ins = pe.matmul(dst, w[a], xa[c], start=first and i == 0, stop=last and i == 2,
                                    skip_group_check=skip)
                return ins

            def wait_g(g):
                if g >= 2:
                    pe.wait_ge(g_freed, n_g_free[g - 2])

            def wait_ring(r):
                if r >= SRING:
                    old = ring_step[r - SRING]
                    if old[0] == "T":
                        pe.wait_ge(exp_done, exp_of_ring[r - SRING])
                    else:
                        pe.wait_ge(smax_done, n_smax[r - SRING])

            def wait_acc(a):
                if a >= 2:
                    pe.wait_ge(acc_freed, n_acc_free[a - 2])

            pe.wait_ge(consts_made, 3)
            pe.wait_ge(ones_made, 1)
            for s in PE:
                kind = s[0]
                if kind == "xtr":
                    _, g, l, b, what, tt = s
                    wait_g(g)
                    pe.wait_ge(xn_done, n_xn[g])
                    for kt in range(KT):
                        last = pe.transpose(g_ring[g % 2][:, kt * P:(kt + 1) * P],
                                            xn[:, kt * P:(kt + 1) * P], ident[:, :])
                    last.then_inc(work_done, 1)
                elif kind == "ctr":
                    _, g, kt = s
                    wait_g(g)
                    phase = ctrs.index(s) // KT
                    pe.wait_ge(norm_done, n_norm[PAIRS * phase + PAIRS - 1])
                    for tt in range(TT):
                        last = pe.transpose(g_ring[g % 2][:, tt * P:(tt + 1) * P],
                                            context[:, tt, kt * P:(kt + 1) * P], ident[:, :])
                    last.then_inc(work_done, 1)
                elif kind == "proj":
                    _, c, g, slot, m = s
                    wait_g(g)
                    pe.wait_ge(split_done, n_split[c])
                    pe.wait_ge(g_freed, x_free_count[s])
                    for kt in range(KT):
                        w = [t[:, c % SPLIT, kt * P:kt * P + m] for t in (w_hi, w_lo)]
                        xa = [t[:, slot, kt, :] for t in (xt_hi, xt_lo)]
                        last = three_passes(g_ring[g % 2][0:m, :], w, xa, kt == 0, kt == KT - 1)
                    last.then_inc(work_done, 1)
                elif kind == "v0":
                    _, c, a, slot = s
                    wait_acc(a)
                    pe.wait_ge(split_done, n_split[c])
                    pe.wait_ge(g_freed, x_free_count[s])
                    for tt in range(TT):
                        for kt in range(KT):
                            w = [t[:, slot, kt, tt * P:(tt + 1) * P] for t in (xt_hi, xt_lo)]
                            xa = [t[:, c % SPLIT, kt * P:(kt + 1) * P] for t in (w_hi, w_lo)]
                            last = three_passes(acc[a % 2][:, tt * P:(tt + 1) * P], w, xa, kt == 0,
                                                kt == KT - 1)
                    last.then_inc(work_done, 1)
                elif kind in ("v1", "out"):
                    if kind == "v1":
                        _, c, a, slot, i = s
                        tiles, first, last_step, rows = (2 * i, 2 * i + 1), i == 0, i == 1, P
                        end = True
                    else:
                        _, c, a, slot, kt, hs, i, rows, first, last_step, end = s
                        tiles = (kt,)
                    if first:
                        wait_acc(a)
                        wait_acc(a + 1)
                    pe.wait_ge(split_done, n_split[c])
                    if s in x_free_count:
                        pe.wait_ge(g_freed, x_free_count[s])
                    if kind == "out" and hs >= 0:
                        pe.wait_ge(hlo_done, n_hlo[hs])
                    for n, kt in enumerate(tiles):
                        col = (n if kind == "v1" else i) * HALF
                        xa = [t[0:rows, c % SPLIT, col:col + HALF] for t in (w_hi, w_lo)]
                        for tt in range(TT):
                            at = slice(tt * P, (tt + 1) * P)
                            if kt >= 0:
                                w = [t[0:rows, slot, kt, at] for t in (xt_hi, xt_lo)]
                            else:
                                w = [t[0:rows, hs % HSPLIT, at] for t in (h_hi, h_lo)]
                            bank = (a + tt // 2) % 2
                            last = three_passes(acc[bank][:, tt % 2 * HALF:(tt % 2 + 1) * HALF], w, xa,
                                                first and n == 0 and tt % 2 == 0,
                                                last_step and n == len(tiles) - 1, skip=True)
                            if last_step and n == len(tiles) - 1 and tt == 1:
                                last.then_inc(work_done, 1)
                    last.then_inc(work_done, 1)
                elif kind == "S":
                    _, r, u, i = s
                    wait_ring(r)
                    if i == 0:
                        octet = u // 4
                        pe.wait_ge(q_here[octet % 2], arrival[("q", octet)])
                        pe.wait_ge(k_here[k_slot_and_head(u, 0)[0]], arrival[("k", octet)])
                    if i in (0, 2):
                        parts = ((i // 2, 3, 0),)
                    elif i in (1, 3):
                        parts = ((i // 2, 2, 0), (i // 2, 0, 3 * P))
                    else:
                        parts = ((0, 1, 0), (1, 1, 2 * P))
                    for j, qt, at in parts:
                        n = (qt + 1) * P
                        ks, kh = k_slot_and_head(u, j)
                        last = pe.matmul(s_ring[r % SRING][:, at:at + n],
                                         q_op[0:QROWS, u // 4 % 2, 2 * (u % 4) + j, qt * P:(qt + 1) * P],
                                         k_op[0:QROWS, ks, kh, 0:n], start=True, stop=True)
                    last.then_inc(ring_made, 1)
                elif kind == "Mt":
                    _, r, u = s
                    wait_ring(r)
                    pe.wait_ge(msplit_done, n_msplit[u])
                    pe.transpose(s_ring[r % SRING][:, :].bitcast(BF16)[0:24, 0:P],
                                 m_parts[:, u % 2, :, :].rearrange("p s g -> p (s g)"), ident16[:, :]
                                 ).then_inc(ring_made, 1)
                elif kind == "T":
                    _, r, j_no, u, i = s
                    wait_ring(r)
                    if i == 0:
                        pe.wait_ge(m_here[u % 2], 16 * (u // 2 + 1))
                    if i in (0, 2):
                        parts = ((i // 2, 0, 0),)
                    elif i in (1, 3):
                        parts = ((i // 2, 1, 0), (i // 2, 3, 3 * P))
                    else:
                        parts = ((0, 2, 0), (1, 2, 2 * P))
                    for j, kt, at in parts:
                        n = T - kt * P
                        ks, kh = k_slot_and_head(u, j)
                        last = pe.matmul(s_ring[r % SRING][:, at:at + n],
                                         k_op[0:MROWS, ks, kh, kt * P:(kt + 1) * P],
                                         q_op[0:MROWS, u // 4 % 2, 2 * (u % 4) + j, kt * P:T],
                                         start=True, stop=True)
                    last.then_inc(ring_made, 1)
                elif kind == "PV":
                    _, u, half = s
                    l, b = PHASES[u // PAIRS]
                    if half == 0:
                        if u % PAIRS == 0:
                            pe.wait_ge(vlo_done, vlo_at[(0, 1) if l == 0 else (1, b)])
                        if u:
                            pe.wait_ge(norm_done, n_norm[u - 1])
                        pe.wait_ge(plo_done, n_plo[5 * u + 4])
                    j = half
                    slot, vh = v_head(u, j)
                    for qt in range(TT):
                        dst = pv_ps[:, (qt * 2 + j) * VW:(qt * 2 + j) * VW + 3 * HD + 1]
                        for kt in range(qt + 1):
                            job, at = ((2 * j, qt * P), (2 * j + 1, (qt - 1) * P),
                                       (4, 2 * P * j + (qt - 2) * P), (2 * j + 1, 3 * P))[kt]
                            ring = (5 * u + job) % PRING
                            for n, part in enumerate((p_hi, p_lo)):
                                last = pe.matmul(dst, part[:, ring, at:at + P],
                                                 v_op[:, slot, kt, vh, 0:3 * HD + 1],
                                                 start=kt == 0 and n == 0, stop=kt == qt and n == 1)
                    if half == 1:
                        last.then_inc(pv_done, 1)
                else:
                    raise AssertionError(kind)


def chunks_of(w, cols, tiles):
    k, n = w.shape
    rows = -(-k // (P * tiles)) * P * tiles
    wide = -(-n // cols) * cols
    full = np.zeros((rows, wide), w.dtype)
    full[:k, :n] = w
    c = full.reshape(rows // (P * tiles), tiles, P, wide // cols, cols)
    return c.transpose(3, 0, 2, 1, 4).reshape(-1, P, 512)


def pack_weights(w):
    wkv = w["L0_attn_Wkv"].reshape(D, G, 2, HD)
    layers = (
        (w["L0_attn_Wq"], wkv[:, :, 0].reshape(D, G * HD), wkv[:, :, 1].reshape(D, G * HD),
         w["L0_ffn_gate_w"].T, w["L0_ffn_up_w"].T, w["L0_attn_Wo"], w["L0_ffn_down_w"].T),
        (w["L1_attn_Wq"].T, w["L1_attn_Wk"].T, w["L1_attn_Wv"].T,
         w["L1_ffn_W_gate"].T, w["L1_ffn_W_up"].T, w["L1_attn_Wo"].T, w["L1_ffn_W_down"].T),
    )
    parts = []
    for l, (q, k, v, gate, up, o, down) in enumerate(layers):
        parts += [chunks_of(q, P, KT), chunks_of(k, P, KT)]
        parts.append(chunks_of(v, P, KT) if l == 0 else chunks_of(v, HALF, 2))
        both = np.stack([chunks_of(gate, P, KT), chunks_of(up, P, KT)], axis=1)
        parts.append(both.reshape(-1, P, 512))
        parts += [chunks_of(o, HALF, 2), chunks_of(down, HALF, 2)]
    return np.ascontiguousarray(np.concatenate(parts))


def kernel(**inputs):
    import concourse.bacc as bacc
    from concourse.bass_utils import run_bass_kernel_spmd

    w = {k: np.asarray(v) for k, v in inputs.items()}
    qk_bias = np.zeros((P, 2, 2, 4), np.float32)
    qk_bias[:, 1, 0] = w["L1_attn_bq"].reshape(4, P).T
    qk_bias[:, 1, 1] = w["L1_attn_bk"].reshape(4, P).T
    arrays = {
        "x": np.ascontiguousarray(w["L0_attn_x"]),
        "weights": pack_weights(w),
        "qk_bias": qk_bias,
        "ln_w": np.ascontiguousarray(w["L0_ffn_ln_w"].reshape(KT, P).T),
        "bv": np.ascontiguousarray(w["L1_attn_bv"]),
        "bo0": np.ascontiguousarray(w["L0_attn_bo"]),
        "bo1": np.ascontiguousarray(w["L1_attn_bo"]),
    }
    nc = bacc.Bacc("TRN2", target_bir_lowering=False, num_devices=1)
    args = [nc.dram_tensor(f"{n}_in", a.shape, F32, kind="ExternalInput").ap() for n, a in arrays.items()]
    qk_scratch = nc.dram_tensor("qk_scratch", (2, P, 3, T), BF16).ap()
    m_scratch = nc.dram_tensor("m_scratch", (2, 24, P), BF16).ap()
    out = nc.dram_tensor("y_out", (B, T, D), F32, kind="ExternalOutput").ap()
    two_layers(nc, *args, qk_scratch, m_scratch, out)
    got = run_bass_kernel_spmd(nc, [{f"{n}_in": a for n, a in arrays.items()}], core_ids=[0])
    return got.results[0]["y_out"]
```

```python
from contextlib import ExitStack

import numpy as np
import concourse.bass as bass
from concourse import mybir

F32 = mybir.dt.float32
F32R = mybir.dt.float32r
BF16 = mybir.dt.bfloat16
F16 = mybir.dt.float16
ALU = mybir.AluOpType
ACT = mybir.ActivationFunctionType
AX = mybir.AxisListType.X

P = 128
B, T, D = 2, 512, 512
H, G, HD = 32, 8, 16
REP = H // G
KT = D // P
TT = T // P
FF = (1792, 1376)
FT = tuple(-(-f // P) for f in FF)
PAIRS = H // 2
SLOTS = PAIRS
PHASES = ((0, 0), (0, 1), (1, 0), (1, 1))
HALF = D // 2
VW = 50
QROWS = 6 * HD
MROWS = QROWS + 3
Q_PARTS = (0, 0, 1, 0, 1, 2)
K_PARTS = (0, 1, 0, 2, 1, 0)
SCALE = 1.0 / HD ** 0.5
EPS = 1e-5
LOWEST = -3.0e38

RAW, SPLIT, HSPLIT, PRING, SRING = 2, 3, 3, 6, 3


def chunk_table():
    names = []
    for l in range(2):
        names += [("q", l, m) for m in range(4)]
        names += [("k", l, m) for m in range(1 if l == 0 else 4)]
        names += [("v", l, m) for m in range(1 if l == 0 else 4)]
        for f in range(FT[l]):
            names += [("g", l, f), ("u", l, f)]
        names += [("o", l, nh, c) for nh in range(2) for c in range(2)]
        names += [("d", l, nh, c) for nh in range(2) for c in range(-(-FT[l] // 2))]
    return {n: i for i, n in enumerate(names)}


PE_US = {"xtr": 0.45, "ctr": 0.45, "proj": 2.6, "v0": 5.1, "v1": 2.62, "out": 1.31, "S": 0.22,
         "Mt": 0.1, "T": 0.22, "PV": 0.55}
ACT_US = {"whi": 0.52, "root": 1.5, "root2": 1.5, "xhi": 0.6, "chi": 0.48, "qhi": 0.48,
          "qmid": 0.52, "vhi": 0.52, "vmid": 0.52, "tanh": 0.48, "exp": 0.48, "phi": 0.52, "hhi": 0.52}
DVE_US = {"stats": 3.0, "rstd": 1.7, "rstd2": 1.2, "xn": 0.34, "xlo": 0.66, "clo": 0.6, "qres": 0.6,
          "vsum": 0.6, "gsum": 0.6, "hmul": 0.6, "xadd": 0.6, "smax": 0.68, "mrow": 0.13,
          "plo": 0.6, "norm": 1.06, "hlo": 0.6}
POOL_US = {"msplit": 1.2, "wlo": 1.25, "qlo": 1.25, "vres": 1.25, "vlo": 1.25, "xbias": 1.25, "mask": 0.34}
SP_US = {"wload": 0.45, "qkout": 0.45, "qkin": 2.7, "mout": 0.45, "min": 0.45, "store": 0.45, "bo1": 0.45}
US = {"pe": PE_US, "act": ACT_US, "dve": DVE_US, "pool": POOL_US, "sp": SP_US}
SIGNAL = {"pe": 0.18, "act": 0.16, "dve": 0.24, "pool": 0.16, "sp": 0.1}
TRANSFER = 2.0
EARLY = 4.0
LATE = 3.0
LOAD_AHEAD = 17.0
NEAR = 0.05
LEAD_JOBS = 0
HEADS = (10, 0, 0, 7)
CTX_AT = 3
QK_AT = 0
S_AT = 0.0
T_AT = 0.15
PV_AT = 0.6
MT_AT = 0.4
LN_EVERY = 2
LN_SLOTS = (9, 9, 10, 10)
V_SLOTS = (11, 13)
X_LOADED = (4.0, 7.0)
NEVER = 1e9


def plan():
    line = {e: [] for e in US}
    busy = {e: [] for e in US}
    table = chunk_table()
    state = {"t": 0.0, "chunk": 0, "g": 0, "acc": 0, "ring": 0, "qk": 0, "hs": 0, "tj": 0, "gate": 0}
    end = {}

    def gap(engine, ready, cost):
        lane = busy[engine]
        i = len(lane)
        while i and lane[i - 1][1] > ready:
            i -= 1
        while i < len(lane) and lane[i][0] < ready + cost:
            ready = max(ready, lane[i][1])
            i += 1
        return ready

    def place(engine, ready, *step):
        cost = US[engine][step[0]]
        start = gap(engine, max(ready, 0.0), cost)
        busy[engine].append((start, start + cost))
        busy[engine].sort()
        line[engine].append((start, len(line[engine]), step))
        return start + cost + SIGNAL[engine]

    def pe_step(ready, *step):
        start = max(state["t"], ready)
        line["pe"].append((start, len(line["pe"]), step))
        state["t"] = start + PE_US[step[0]]
        return state["t"] + SIGNAL["pe"]

    def take(name):
        state[name] += 1
        return state[name] - 1

    def at(*name):
        return end.get(name if len(name) > 1 else name[0], NEVER)

    def after(*name):
        return end.get(name if len(name) > 1 else name[0], 0.0)

    def freed(ring, n, depth):
        return at(ring, n - depth) if n >= depth else 0.0

    def chunk_ready():
        c = state["chunk"]
        load = max(after("split", c - RAW), state["t"] - LOAD_AHEAD)
        whi = gap("act", max(load + TRANSFER, after("used", c - SPLIT)), ACT_US["whi"])
        return gap("pool", whi + ACT_US["whi"] + SIGNAL["act"], POOL_US["wlo"]) + POOL_US["wlo"] + SIGNAL["pool"]

    def chunk(name):
        c = take("chunk")
        load = place("sp", max(after("split", c - RAW), state["t"] - LOAD_AHEAD), "wload", c, table[name])
        whi = place("act", max(load + TRANSFER, after("used", c - SPLIT)), "whi", c)
        end["split", c] = place("pool", whi, "wlo", c)
        return c

    def ln_stats(l, b):
        ready = after("x_final", l - 1, b) if l else X_LOADED[b]
        stats = place("dve", max(ready, after("ln_scratch")), "stats", l, b)
        done = end["stats", l, b, "x"] = place("dve", place("act", stats, "root", l, b), "rstd", l, b)
        if l == 0:
            done = end["stats", l, b, "n"] = place("dve", place("act", done, "root2", l, b), "rstd2", l, b)
        end["ln_scratch"] = done

    def ln_tile(l, b, kind, slot, tt):
        g = take("g")
        xn = place("dve", max(at("stats", l, b, kind), after("xtr")), "xn", l, b, kind, tt, g)
        e = end["xtr"] = pe_step(max(xn, after("g", g - 2)), "xtr", g, l, b, kind, tt)
        hi = place("act", max(e, after("x_read", slot)), "xhi", g, kind, slot, tt)
        end["g", g] = end["x", slot] = place("dve", hi, "xlo", g, kind, slot, tt)

    def xn_ready(l, b, kind):
        ready = max(at("stats", l, b, kind), after("xtr"))
        return ready if ready == NEVER else gap("dve", ready, DVE_US["xn"]) + DVE_US["xn"] + SIGNAL["dve"]

    def ctx_tile(ph, slot, kt):
        g = take("g")
        e = pe_step(max(after("norm"), after("g", g - 2)), "ctr", g, kt)
        if kt == KT - 1:
            end["ctr", ph] = e
        hi = place("act", max(e, after("x_read", slot)), "chi", g, slot, kt)
        end["g", g] = end["x", slot] = place("dve", hi, "clo", g, slot, kt)

    def proj_ready(xslot):
        return max(after("g", state["g"] - 2), at("x", xslot), chunk_ready())

    def proj(name, xslot, m):
        g, c = take("g"), chunk(name)
        e = pe_step(max(after("g", g - 2), at("x", xslot), end["split", c]), "proj", c, g, xslot, m)
        end["used", c] = end["x_read", xslot] = e
        return g, e

    def qk_job(kind, l, b, m, xslot, octet):
        n = take("qk")
        g, e = proj((kind, l, m), xslot, P)
        hi = place("act", max(e, after("qkout", n - 2)), "qhi", n, g, kind, l, m)
        res = end["g", g] = place("dve", max(hi, after("rest")), "qres", n, g, kind, l, m)
        lo = end["rest"] = place("pool", place("act", res, "qmid", n), "qlo", n)
        end["qkout", n] = place("sp", max(lo, after("qkin", n - 2)), "qkout", n) + TRANSFER
        if kind == "q":
            used = at("T", 4 * (octet - 2) + 3) if octet >= 2 else 0.0
        else:
            used = at("T", {8: 15, 9: 31}.get(octet, 4 * (octet - 2) + 3)) if l else 0.0
        assert used < NEVER
        end["qkin", n] = end[kind, octet] = place("sp", max(end["qkout", n], used), "qkin", n, kind, l, b,
                                                  octet) + TRANSFER

    def qk_ready(kind, l, xslot, octet):
        last = 4 * (octet - 2) + 3
        if kind == "k" and l:
            last = {8: 15, 9: 31}.get(octet, last)
        if (kind == "q" and octet >= 2 or kind == "k" and l) and at("T", last) == NEVER:
            return NEVER
        return proj_ready(xslot)

    def v_job(l, b, xslot, part):
        a = take("acc")
        free = max(freed("acc", a, 2), at("x", xslot))
        if l == 0:
            c = chunk(("v", 0, 0))
            e = end["used", c] = end["x_read", xslot] = pe_step(max(free, end["split", c]), "v0", c, a, xslot)
            accs = (a,)
        else:
            a2 = take("acc")
            free = max(free, freed("acc", a2, 2))
            accs = (a, a2)
            for i in range(2):
                c = chunk(("v", 1, part * 2 + i))
                e = pe_step(max(free, end["split", c]), "v1", c, a, xslot, i)
                end["used", c] = end["x_read", xslot] = e
        used = at("PV", 2 * PAIRS - 1) if (l, b) == (1, 1) else 0.0
        for i, x in enumerate(accs):
            done = end["acc", x] = place("dve", max(e, after("rest")), "vsum", x, l, b, part, i)
            done = place("act", max(done, used), "vhi", x, l, b, part, i)
            done = place("pool", done, "vres", x, l, b, part, i)
            done = place("act", done, "vmid", x, l, b, part, i)
            end["v", l, b] = end["rest"] = place("pool", done, "vlo", x, l, b, part, i)

    def v_ready(xslot):
        a = state["acc"]
        return max(freed("acc", a, 2), freed("acc", a + 1, 2), at("x", xslot), chunk_ready())

    def ffn_job(l, xslot, f, which):
        m = min(P, FF[l] - f * P)
        g, e = proj((which, l, f), xslot, m)
        if which == "g":
            n = take("gate")
            done = place("act", max(e, after("gate", n - 2)), "tanh", n, g, m)
            end["g", g] = end["gsum", n] = place("dve", done, "gsum", n, g, m)
        else:
            n = state["gate"] - 1
            free = max(e, end["gsum", n], after("h_used"))
            end["g", g] = end["gate", n] = end["h"] = place("dve", free, "hmul", n, g, f, m)

    def out_ready(l, slot, kind, tile, i, first):
        r = max(freed("acc", state["acc"], 2), freed("acc", state["acc"] + 1, 2)) if first else 0.0
        r = max(r, at("x", slot) if kind == "o" else after("h"))
        if i == 0:
            r = max(r, chunk_ready())
        if kind == "d":
            hi = gap("act", max(end["h"], after("h_slot", state["hs"] - HSPLIT)), ACT_US["hhi"])
            r = max(r, gap("dve", hi + ACT_US["hhi"] + SIGNAL["act"], DVE_US["hlo"]) + DVE_US["hlo"] + SIGNAL["dve"])
        return r

    def out_tile(l, b, slot, nh, kind, tile, i, first, last, chunk_done):
        ready, rows, h = 0.0, P, -1
        if first:
            state["a"] = take("acc")
            take("acc")
            ready = max(freed("acc", state["a"], 2), freed("acc", state["a"] + 1, 2))
        if i == 0:
            state["w"] = chunk(("o" if kind == "o" else "d", l, nh, tile // 2))
        w = state["w"]
        ready = max(ready, end["split", w], at("x", slot) if kind == "o" else 0.0)
        if kind == "d":
            h, rows = take("hs"), min(P, FF[l] - tile * P)
            hi = place("act", max(end["h"], after("h_slot", h - HSPLIT)), "hhi", h, tile, rows)
            lo = place("dve", hi, "hlo", h, tile, rows)
            ready = max(ready, lo)
            if nh == 1 and tile == FT[l] - 1:
                end["h_used"] = lo
        e = pe_step(ready, "out", w, state["a"], slot, tile if kind == "o" else -1, h, i, rows,
                    first, last, chunk_done)
        if kind == "d":
            end["h_slot", h] = e
        else:
            end["x_read", slot] = e
        if chunk_done:
            end["used", w] = e
        else:
            end["used", w] = NEVER
        if last:
            for i in range(2):
                a = state["a"] + i
                done = end["acc", a] = place("dve", e, "xadd", a, l, b, nh, i)
                done = end["x_final", l, b] = place("pool", max(done, after("bo1") if l else 0.0),
                                                    "xbias", a, l, b, nh, i)
                if nh == 0:
                    end["x_final", l, b] = NEVER
                if l == 1:
                    place("sp", done, "store", a, b, nh, i)
                elif b == 1 and nh == 1 and i == 1:
                    end["bo1"] = place("sp", done, "bo1") + TRANSFER

    def score_ready(u, i):
        if u >= 2 and at("msplit", u - 2) == NEVER:
            return NEVER
        return max(after("ring", state["ring"] - SRING), at("q", u // 4),
                   at("k", u // 4 if u >= 2 * PAIRS else 0), at("k", 4) if u < 2 * PAIRS else 0.0)

    def score(u, i):
        r = take("ring")
        operands = max(at("q", u // 4), at("k", u // 4 if u >= 2 * PAIRS else 0))
        e = pe_step(max(after("ring", r - SRING), operands), "S", r, u, i)
        end["ring", r] = place("dve", max(e, after("msplit", u - 2)), "smax", r, u, i)
        if i == 4:
            end["msplit", u] = place("pool", max(end["ring", r], after("Mt", u - 2)), "msplit", u)

    def mtrans_ready(u):
        return max(after("ring", state["ring"] - SRING), at("msplit", u))

    def mtrans(u):
        r = take("ring")
        e = end["Mt", u] = pe_step(max(after("ring", r - SRING), end["msplit", u]), "Mt", r, u)
        done = end["ring", r] = place("dve", max(e, after("mout", u - 2)), "mrow", r, u)
        done = end["mout", u] = place("sp", max(done, after("min", u - 2)), "mout", u) + TRANSFER
        end["min", u] = place("sp", max(done, after("T", u - 8)), "min", u) + TRANSFER

    def trans_ready(u, i):
        j = state["tj"]
        if j >= PRING and at("PV", (j - PRING) // 5) == NEVER:
            return NEVER
        return max(after("ring", state["ring"] - SRING), at("min", u), after("plo", j - 2) - 0.4)

    def trans(u, i):
        r, j = take("ring"), take("tj")
        e = end["T", u] = pe_step(max(after("ring", r - SRING), at("min", u)), "T", r, j, u, i)
        if i < 4:
            end["T", u] = NEVER
        done = end["ring", r] = place("act", max(e, after("plo", j - 2)), "exp", r, j, i)
        done = place("pool", done, "mask", j, i)
        done = place("act", max(done, after("PV", (j - PRING) // 5)), "phi", j)
        end["plo", j] = place("dve", done, "plo", j)

    def pv_ready(u):
        v = max(at("v", 0, 0), at("v", 0, 1)) if u < 2 * PAIRS else at("v", *PHASES[u // PAIRS])
        if u >= PAIRS and u % PAIRS == 0:
            v = max(v, at("ctr", u // PAIRS - 1))
        return max(v, at("plo", 5 * u + 4), after("norm"))

    def pv(u, half):
        e = pe_step(0.0 if half else pv_ready(u), "PV", u, half)
        if half == 1:
            end["PV", u] = e
            end["norm"] = end["norm", u] = place(
                "dve", e, "norm", u)

    def w_ln(l, b, kind, slot, stats):
        w = [(0.1, lambda: at("x_final", l - 1, b) if l else 0.0, lambda: ln_stats(l, b))] if stats else []
        return w + [(0.5, lambda: max(xn_ready(l, b, kind), after("g", state["g"] - 2)),
                     lambda tt=tt: ln_tile(l, b, kind, slot, tt)) for tt in range(TT)]

    def w_v(l, b, xslot):
        return [(2.6 if l == 0 else 5.2, lambda: NEVER if (l, b) == (1, 1) and at("PV", 2 * PAIRS - 1) == NEVER
                 else v_ready(xslot), lambda part=part: v_job(l, b, xslot, part)) for part in range(1 + l)]

    def w_qk(kind, l, b, m, xslot, octet):
        return [(2.6, lambda: qk_ready(kind, l, xslot, octet), lambda: qk_job(kind, l, b, m, xslot, octet))]

    def w_octet(ph, o, xslot):
        l, b = PHASES[ph]
        return [w for kind in ("qk" if l else "q") for w in w_qk(kind, l, b, o, xslot, 4 * ph + o)]

    def w_ffn(l, xslot):
        return [(2.6, lambda: proj_ready(xslot), lambda f=f, w=w: ffn_job(l, xslot, f, w))
                for f in range(FT[l]) for w in "gu"]

    def w_ctx(ph, slot):
        return [(0.9, lambda: max(at("norm", PAIRS * ph + PAIRS - 1), after("g", state["g"] - 2)),
                 lambda kt=kt: ctx_tile(ph, slot, kt)) for kt in range(KT)]

    def w_out(ph, slot):
        l, b = PHASES[ph]
        halves = []
        for nh in range(2):
            w = []
            o, d = [("o", k) for k in range(KT)], [("d", k) for k in range(FT[l])]
            tiles = o + d if nh else d + o
            for n, (k, tile) in enumerate(tiles):
                i, count = tile % 2, KT if k == "o" else FT[l]
                w.append((1.3, lambda k=k, tile=tile, i=i, n=n: out_ready(l, slot, k, tile, i, n == 0),
                          lambda k=k, tile=tile, i=i, n=n, nh=nh, chunk_done=i == 1 or tile == count - 1:
                          out_tile(l, b, slot, nh, k, tile, i, n == 0, n == len(tiles) - 1, chunk_done)))
            if nh == 0:
                w[HEADS[ph] + CTX_AT:HEADS[ph] + CTX_AT] = w_ctx(ph, slot)
            halves += w
        return halves

    ln_1, ln_n = w_ln(0, 1, "x", 1, True), w_ln(0, 0, "n", 1, False)
    q, k0, k1 = w_octet(0, 0, 0), w_qk("k", 0, 0, 0, 0, 0), w_qk("k", 0, 1, 0, 1, 4)
    prologue = (w_ln(0, 0, "x", 0, True) + ln_1[:1] + q + ln_1[1:3] + k0 + ln_1[3:] + k1
                + w_v(0, 1, 1) + ln_n[:1] + w_v(0, 0, 0) + ln_n[1:])
    ffn00 = w_ffn(0, 1)
    fill = list(prologue)
    starts = [sum(c for c, _, _ in fill)]
    starts += [starts[0] + 1.3 * LEAD_JOBS]
    head, ffn00 = ffn00[:LEAD_JOBS], ffn00[LEAD_JOBS:]
    fill += head
    starts.append(sum(c for c, _, _ in fill))

    def out_then_ln(w, ln):
        cut = len(w) - 4 * LN_EVERY
        out = w[:cut]
        for i in range(4):
            out += w[cut + i * LN_EVERY:cut + (i + 1) * LN_EVERY] + ln[i:i + 1]
        return out

    outs = [w_out(ph, slot) for ph, slot in enumerate((1, 1, 0, 0))]
    heads, outs = [w[:n] for w, n in zip(outs, HEADS)], [w[n:] for w, n in zip(outs, HEADS)]
    free = [
        ffn00 + heads[0],
        out_then_ln(outs[0], w_ln(0, 1, "n", 1, False)) + w_ffn(0, 1) + heads[1],
        outs[1] + w_ffn(1, 0) + heads[2],
        outs[2] + w_ffn(1, 1) + heads[3],
    ]
    lns = [w_ln(0, 1, "x", 0, False), w_ln(1, 0, "x", 0, True), w_ln(1, 1, "x", 1, True)]
    due = [{}, {}, {}, {}]
    for ph, w in enumerate(lns):
        for i, step in enumerate(w[-4:]):
            due[ph].setdefault(LN_SLOTS[i], []).append(step)
        if len(w) > 4:
            due[ph].setdefault(LN_SLOTS[0] - 1, []).insert(0, w[0])
    for ph in (1, 2):
        for slot, w in zip(V_SLOTS, w_v(1, ph - 1, ph - 1)):
            due[ph].setdefault(slot, []).append(w)
    xslot_of = (0, 0, 0, 1)
    pinned = []
    for ph in range(4):
        for o in range(4):
            nxt = (ph, o + 1) if o < 3 else (ph + 1, 0)
            if nxt[0] < 4:
                due[ph][4 * o + QK_AT] = due[ph].get(4 * o + QK_AT, []) + w_octet(nxt[0], nxt[1], xslot_of[nxt[0]])
        total = sum(w[0] for w in free[ph]) + sum(w[0] for ws in due[ph].values() for w in ws)
        fill += free[ph]
        t0 = starts[-1]
        for s in range(SLOTS):
            starts.append(t0 + total * (s + 1) / SLOTS)
            ws = due[ph].get(s, [])
            pinned += [(starts[-2] + (starts[-1] - starts[-2]) * i / len(ws), ready, run, cost)
                       for i, (cost, ready, run) in enumerate(ws)]
    fill += outs[3]
    starts += [starts[-1] + 5.0, starts[-1] + 10.0]

    queues = {"S": [], "T": [], "PV": [], "Mt": [], "pinned": pinned}
    units = 4 * PAIRS
    for p in range(-2, units + 1):
        t0, t1 = starts[p + 2], starts[p + 3]
        where = lambda f: t0 + (t1 - t0) * f
        if p + 2 < units:
            queues["S"] += [(where(S_AT + i / 5), lambda u=p + 2, i=i: score_ready(u, i),
                             lambda u=p + 2, i=i: score(u, i)) for i in range(5)]
        if -1 <= p < units - 1:
            queues["Mt"].append((where(MT_AT), lambda u=p + 1: mtrans_ready(u), lambda u=p + 1: mtrans(u)))
        if 0 <= p < units:
            queues["T"] += [(where(T_AT + i / 5), lambda u=p, i=i: trans_ready(u, i),
                             lambda u=p, i=i: trans(u, i)) for i in range(5)]
        if 1 <= p <= units:
            queues["PV"].append((where(PV_AT), lambda u=p - 1: pv_ready(u),
                                 lambda u=p - 1: (pv(u, 0), pv(u, 1))))
    progress = 0.0
    while fill or any(queues.values()):
        t = state["t"]
        heads = [(q[0][0], q[0][1](), name) for name, q in queues.items() if q]
        can = fill[0][1]() if fill else NEVER
        due_now = [h for h in heads if h[0] <= progress and h[1] <= t + NEAR]
        late = [h for h in heads if h[0] <= progress - LATE and h[1] < NEVER]
        soon = [h for h in heads if h[0] <= progress + EARLY and h[1] <= t]
        if due_now:
            pick = min(due_now)[2]
        elif late and min(late)[1] < max(can, t + 1.5):
            pick = min(late)[2]
        elif can <= t + NEAR:
            pick = None
        elif soon:
            pick = min(soon)[2]
        else:
            near = [(r, name) for pos, r, name in heads if r < NEVER and (pos <= progress + EARLY or can == NEVER)]
            pick = min(near)[1] if near and min(near)[0] < can else None
            assert pick or can < NEVER, (heads, can)
        if pick:
            step = queues[pick].pop(0)
            step[2]()
            progress += step[3] if pick == "pinned" else 0.0
        else:
            cost, _, run = fill.pop(0)
            run()
            progress += cost
    return {e: [s for _, _, s in sorted(x, key=lambda x: x[:2])] for e, x in line.items()}



def numbered(steps, *kinds):
    out = {}
    for s in steps:
        if s[0] in kinds:
            out[s] = len(out) + 1
    return out


def by(numbers, *at):
    return {tuple(s[i] for i in at) if len(at) > 1 else s[at[0]]: n for s, n in numbers.items()}


def two_layers(nc, x_in, weights, qk_bias, ln_w, bv, bo0, bo1, qk_scratch, m_scratch, out):
    steps = plan()
    PE, SE, VE, GP, SP = (steps[e] for e in ("pe", "act", "dve", "pool", "sp"))

    n_split = by(numbered(GP, "wlo"), 1)
    n_whi = by(numbered(SE, "whi"), 1)
    n_g_made, n_acc_made, n_chunk_used, n_out_used, count = {}, {}, {}, {}, 0
    for s in PE:
        if s[0] in ("xtr", "ctr"):
            count += 1
            n_g_made[s[1]] = count
        elif s[0] == "proj":
            count += 1
            n_g_made[s[2]] = n_chunk_used[s[1]] = count
        elif s[0] == "v0":
            count += 1
            n_acc_made[s[2]] = n_chunk_used[s[1]] = count
        elif s[0] in ("v1", "out"):
            if s[4] == 1 if s[0] == "v1" else s[9]:
                count += 1
                n_acc_made[s[2]] = count
                n_acc_made[s[2] + 1] = count + 1
            count += 1
            n_chunk_used[s[1]] = count
            if s[0] == "out" and s[5] >= 0:
                n_out_used[s[5]] = count
    g_free = numbered(VE, "qres", "gsum", "hmul", "xlo", "clo")
    n_g_free = {s[1] if s[0] in ("xlo", "clo") else s[2]: n for s, n in g_free.items()}
    n_acc_free = by(numbered(VE, "vsum", "xadd"), 1)
    ring_step = {s[1]: s for s in PE if s[0] in ("S", "T", "Mt")}
    n_ring = by(numbered(PE, "S", "T", "Mt"), 1)
    n_smax = by(numbered(VE, "smax", "mrow"), 1)
    n_exp = by(numbered(SE, "exp"), 2)
    exp_of_ring = {s[1]: n_exp[s[2]] for s in SE if s[0] == "exp"}
    last_smax = {s[2]: n_smax[s[1]] for s in VE if s[0] == "smax" and s[3] == 4}
    mrow_of = {s[2]: n_smax[s[1]] for s in VE if s[0] == "mrow"}
    t_of = {(s[3], s[4]): n_ring[s[1]] for s in PE if s[0] == "T"}
    mt_of = {s[2]: n_ring[s[1]] for s in PE if s[0] == "Mt"}
    n_mask = by(numbered(GP, "mask"), 1)
    n_phi = by(numbered(SE, "phi"), 1)
    n_plo = by(numbered(VE, "plo"), 1)
    n_pv = {s[1]: i + 1 for i, s in enumerate(s for s in PE if s[0] == "PV" and s[2] == 1)}
    n_norm = by(numbered(VE, "norm"), 1)
    n_msplit = by(numbered(GP, "msplit"), 1)
    n_qhi = by(numbered(SE, "qhi"), 1)
    n_qmid = by(numbered(SE, "qmid"), 1)
    n_qlo = by(numbered(GP, "qlo"), 1)
    n_vhi = by(numbered(SE, "vhi"), 1)
    n_vmid = by(numbered(SE, "vmid"), 1)
    n_vlo = by(numbered(GP, "vlo"), 1)
    n_vres = by(numbered(GP, "vres"), 1)
    n_xbias = by(numbered(GP, "xbias"), 1)
    n_xbias_l0 = max(n_xbias[s[1]] for s in GP if s[0] == "xbias" and s[2] == 0)
    n_tanh = by(numbered(SE, "tanh"), 1)
    n_xhi = by(numbered(SE, "xhi", "chi"), 1)
    n_hhi = by(numbered(SE, "hhi"), 1)
    n_hlo = by(numbered(VE, "hlo"), 1)
    n_xn = by(numbered(VE, "xn"), 5)
    n_stats = by(numbered(VE, "stats", "rstd", "rstd2"), 0, 1, 2)
    n_root = by(numbered(SE, "root", "root2"), 0, 1, 2)
    arrival, qk_read, seen = {}, {}, {}
    for s in SP:
        if s[0] == "qkin":
            _, n, what, l, b, octet = s
            slots = (0, 1) if what == "k" and l == 0 else (octet % 2,)
            qk_read[n] = []
            for slot in slots:
                seen[(what, slot)] = seen.get((what, slot), 0) + 6 * 16
                arrival[(what, octet)] = seen[(what, slot)]
                qk_read[n].append((what, slot, seen[(what, slot)]))
            if len(slots) == 2:
                for o in range(8):
                    arrival[("k", o)] = seen[("k", 0)]
    vlo_at = {(s[2], s[3]): n_vlo[s[1]] for s in GP if s[0] == "vlo"}

    with ExitStack() as ctx:
        def sb(name, shape, dt):
            return ctx.enter_context(nc.sbuf_tensor(name, shape, dt))

        def sem(name):
            return ctx.enter_context(nc.semaphore(name))

        x = sb("x", [P, B * TT, D], F32)
        xt_hi = sb("xt_hi", [P, 2, KT, T], F32R)
        xt_lo = sb("xt_lo", [P, 2, KT, T], F32R)
        h = sb("h", [P, FT[0], T], F32)
        h_hi = sb("h_hi", [P, HSPLIT, T], F32R)
        h_lo = sb("h_lo", [P, HSPLIT, T], F32R)
        w_raw = sb("w_raw", [P, RAW, 512], F32)
        w_hi = sb("w_hi", [P, SPLIT, 512], F32R)
        w_lo = sb("w_lo", [P, SPLIT, 512], F32R)
        q_op = sb("q_op", [MROWS, 2, 8, T], BF16)
        k_op = sb("k_op", [MROWS, 2, 8, T], BF16)
        v_op = sb("v_op", [P, 2, TT, H, VW], BF16)
        context = sb("context", [P, TT, D], F32)
        p32 = sb("p32", [P, 2, 512], F32)
        p_hi = sb("p_hi", [P, PRING, 512], F16)
        p_lo = sb("p_lo", [P, PRING, 512], F16)
        qk_parts = sb("qk_parts", [P, 2, 3, T], BF16)
        rest = sb("rest", [P, 512], F32)
        xn = sb("xn", [P, D], F32)
        gate = sb("gate", [P, 2, T], F32)
        causal = sb("causal", [P, 512], BF16)
        ident = sb("ident", [P, P], F32)
        ident16 = sb("ident16", [P, P], BF16)
        bv_all = sb("bv_all", [P, D], F32)
        bo_all = sb("bo_all", [P, D], F32)
        biases = sb("biases", [P, 2, 2, 4], F32)
        lnw = sb("lnw", [P, KT], F32)
        maxima = sb("maxima", [P, 2, 8], F32)
        m_rest = sb("m_rest", [P, 8], F32)
        m_parts = sb("m_parts", [P, 2, 3, 8], BF16)
        m_rows = sb("m_rows", [24, 2, P], BF16)
        pv_sum = sb("pv_sum", [P, TT, 2, HD], F32)
        recip = sb("recip", [P, TT, 2], F32)
        bn = sb("bn", [P, TT, 6], F32)
        mv = sb("mv", [P, B, TT, 2], F32)
        ve = sb("ve", [P, TT], F32)
        ms = sb("ms", [P, TT], F32)
        root = sb("root", [P, TT], F32)
        root2 = sb("root2", [P, TT], F32)
        newton = sb("newton", [P, TT], F32)
        rstd = sb("rstd", [P, B, TT], F32)
        rstd_n = sb("rstd_n", [P, B, TT], F32)

        s_ring = [ctx.enter_context(nc.psum_tensor(f"s_ring{i}", [P, 512], F32)) for i in range(SRING)]
        g_ring = [ctx.enter_context(nc.psum_tensor(f"g_ring{i}", [P, 512], F32)) for i in range(2)]
        acc = [ctx.enter_context(nc.psum_tensor(f"acc{i}", [P, 512], F32)) for i in range(2)]
        pv_ps = ctx.enter_context(nc.psum_tensor("pv_ps", [P, 512], F32))

        raw_here = [sem(f"raw_here{i}") for i in range(RAW)]
        x_here = [sem(f"x_here{i}") for i in range(B * TT)]
        consts_here = sem("consts_here")
        bo_here = sem("bo_here")
        consts_made = sem("consts_made")
        ones_made = sem("ones_made")
        whi_done, split_done, work_done = sem("whi_done"), sem("split_done"), sem("work_done")
        g_freed, acc_freed = sem("g_freed"), sem("acc_freed")
        ring_made, smax_done, exp_done = sem("ring_made"), sem("smax_done"), sem("exp_done")
        mask_done, phi_done, plo_done = sem("mask_done"), sem("phi_done"), sem("plo_done")
        pv_done, norm_done, msplit_done = sem("pv_done"), sem("norm_done"), sem("msplit_done")
        qhi_done, qmid_done, qlo_done = sem("qhi_done"), sem("qmid_done"), sem("qlo_done")
        vhi_done, vmid_done, vlo_done = sem("vhi_done"), sem("vmid_done"), sem("vlo_done")
        vres_done = sem("vres_done")
        tanh_done, xhi_done = sem("tanh_done"), sem("xhi_done")
        hhi_done, hlo_done = sem("hhi_done"), sem("hlo_done")
        xn_done, stats_done, root_done = sem("xn_done"), sem("stats_done"), sem("root_done")
        dve_chain, pool_chain = sem("dve_chain"), sem("pool_chain")
        qk_out = [sem(f"qk_out{i}") for i in range(2)]
        q_here = [sem(f"q_here{i}") for i in range(2)]
        k_here = [sem(f"k_here{i}") for i in range(2)]
        m_out = [sem(f"m_out{i}") for i in range(2)]
        m_here = [sem(f"m_here{i}") for i in range(2)]
        xbias_done = sem("xbias_done")
        stored = sem("stored")
        block = ctx.enter_context(nc.Block())

        hmul_of_gate = {s[1]: g_free[s] for s in VE if s[0] == "hmul"}
        gsum_of_gate = {s[1]: g_free[s] for s in VE if s[0] == "gsum"}
        qk_g = {s[1]: s[2] for s in SE if s[0] == "qhi"}
        xtr_made = {n_xn[s[1]]: n_g_made[s[1]] for s in PE if s[0] == "xtr"}
        x_final = {}
        for s in VE:
            if s[0] == "xadd":
                x_final[(s[2], s[3])] = max(n_xbias[s[1]], x_final.get((s[2], s[3]), 0))
        ctrs = [s for s in PE if s[0] == "ctr"]
        ctx_used = {i: n_g_made[ctrs[4 * i + 3][1]] for i in range(4)}
        v_before = {(0, 0): None, (0, 1): None, (1, 0): None, (1, 1): n_pv[2 * PAIRS - 1]}
        rest_before, before = {}, None
        for s in VE:
            if s[0] in ("qres", "vsum"):
                rest_before[s] = before
                before = (qlo_done, n_qlo[s[1]]) if s[0] == "qres" else (vlo_done, n_vlo[s[1]])
        splits = [s for s in VE if s[0] == "hlo"]
        tiles = [s for s in VE if s[0] == "hmul"]
        f_before, last_hmul = {}, {}
        per_phase = [2 * FT[l] for l, _ in PHASES]
        for ph in range(4):
            mine = tiles[sum(FT[l] for l, _ in PHASES[:ph]):][:FT[PHASES[ph][0]]]
            for s in mine:
                f_before[s] = (hlo_done, sum(per_phase[:ph])) if ph else None
            for s in splits[sum(per_phase[:ph]):][:per_phase[ph]]:
                last_hmul[s[1]] = g_free[mine[-1]]

        reads = {0: None, 1: None}
        x_last_read = {}
        x_free_count = {}
        writes = {0: 0, 1: 0}
        slot_of_g = {s[1]: s[3] if s[0] == "xhi" else s[2] for s in SE if s[0] in ("xhi", "chi")}
        for s in PE:
            if s[0] in ("xtr", "ctr"):
                g = s[1]
                slot = slot_of_g[g]
                x_last_read[g] = reads[slot]
                writes[slot] = n_g_free[g]
            elif s[0] == "proj":
                reads[s[3]] = n_g_made[s[2]]
                x_free_count[s] = writes[s[3]]
            elif s[0] in ("v0", "v1"):
                reads[s[3]] = n_chunk_used[s[1]]
                x_free_count[s] = writes[s[3]]
            elif s[0] == "out" and s[4] >= 0:
                reads[s[3]] = n_chunk_used[s[1]]
                x_free_count[s] = writes[s[3]]

        def k_slot_and_head(u, j):
            head = 2 * (u % PAIRS) + j
            if u < 2 * PAIRS:
                return u // PAIRS, head // REP
            return u // 4 % 2, head % 8

        def v_head(u, j):
            l, b = PHASES[u // PAIRS]
            head = 2 * (u % PAIRS) + j
            if l == 1:
                return b, head
            from_batch, group = head // REP % 2, b * (G // 2) + head // (2 * REP)
            return 1, G * from_batch + group

        def v_view(l, b, part, i, piece):
            if l == 0:
                return v_op[:, 1, :, G * b:G * b + G, piece * HD:(piece + 1) * HD]
            heads = slice(part * 16, part * 16 + 16)
            return v_op[:, b, 2 * i:2 * i + 2, heads, piece * HD:(piece + 1) * HD]

        def v_like(flat, l):
            return flat.rearrange("p (t h d) -> p t h d", t=TT if l == 0 else 2, d=HD)

        first_loads = [s for s in SP if s[0] == "wload" and s[1] < RAW]

        @block.sync
        def _(sp):
            def load_weights(s):
                _, c, at = s
                if c >= RAW:
                    sp.wait_ge(split_done, n_split[c - RAW])
                sp.dma_start(w_raw[:, c % RAW, :], weights[at]).then_inc(raw_here[c % RAW], 16)

            for b in range(B):
                for tt in range(TT):
                    sp.dma_start(x[:, b * TT + tt, :], x_in[b, tt * P:(tt + 1) * P, :]
                                 ).then_inc(x_here[b * TT + tt], 16)
                if b == 0:
                    for s in first_loads:
                        load_weights(s)
                    sp.dma_start(biases[:, :, :, :], qk_bias).then_inc(consts_here, 16)
                    sp.dma_start(lnw[:, :], ln_w).then_inc(consts_here, 16)
            sp.dma_start(bv_all[:, :], bv.unsqueeze(0).to_broadcast([P, D])).then_inc(consts_here, 16)
            sp.dma_start(bo_all[:, :], bo0.unsqueeze(0).to_broadcast([P, D])).then_inc(bo_here, 16)
            stores = 0
            for s in SP:
                kind = s[0]
                if kind == "wload":
                    if s not in first_loads:
                        load_weights(s)
                elif kind == "qkout":
                    n = s[1]
                    sp.wait_ge(qlo_done, n_qlo[n])
                    if n >= 2:
                        for what, slot, count in qk_read[n - 2]:
                            sp.wait_ge((q_here if what == "q" else k_here)[slot], count)
                    sp.dma_start(qk_scratch[n % 2], qk_parts[:, n % 2, :, :]).then_inc(qk_out[n % 2], 16)
                elif kind == "qkin":
                    _, n, what, l, b, octet = s
                    sp.wait_ge(qk_out[n % 2], 16 * (n // 2 + 1))
                    dst, parts, here = (q_op, Q_PARTS, q_here) if what == "q" else (k_op, K_PARTS, k_here)
                    if what == "q" and octet >= 2:
                        sp.wait_ge(ring_made, t_of[(4 * (octet - 2) + 3, 4)])
                    if what == "k" and l == 1:
                        last = 15 if octet == 8 else 31 if octet == 9 else 4 * (octet - 2) + 3
                        sp.wait_ge(ring_made, t_of[(last, 4)])
                    rows = qk_scratch[n % 2].rearrange("(h d) s t -> d h s t", d=HD)
                    for g, part in enumerate(parts):
                        to = dst[g * HD:(g + 1) * HD]
                        if what == "k" and l == 0:
                            for slot in range(2):
                                sp.dma_start(to[:, slot, b:8:2, :], rows[:, 4 * slot:4 * slot + 4, part, :]
                                             ).then_inc(here[slot], 16)
                        else:
                            sp.dma_start(to[:, octet % 2, :, :], rows[:, :, part, :]
                                         ).then_inc(here[octet % 2], 16)
                elif kind == "mout":
                    u = s[1]
                    sp.wait_ge(smax_done, mrow_of[u])
                    if u >= 2:
                        sp.wait_ge(m_here[u % 2], 16 * (u // 2))
                    sp.dma_start(m_scratch[u % 2], m_rows[:, u % 2, :]).then_inc(m_out[u % 2], 16)
                elif kind == "min":
                    u = s[1]
                    sp.wait_ge(m_out[u % 2], 16 * (u // 2 + 1))
                    if u >= 8:
                        sp.wait_ge(ring_made, t_of[(u - 8, 4)])
                    h0 = 2 * (u % 4)
                    sp.dma_start(q_op[QROWS:MROWS, u // 4 % 2, h0:h0 + 2, :].rearrange("c h t -> c (h t)"),
                                 m_scratch[u % 2].rearrange("(c r) t -> c (r t)", c=3)
                                 ).then_inc(m_here[u % 2], 16)
                elif kind == "bo1":
                    sp.wait_ge(xbias_done, n_xbias_l0)
                    sp.dma_start(bo_all[:, :], bo1.unsqueeze(0).to_broadcast([P, D])).then_inc(bo_here, 16)
                elif kind == "store":
                    _, a, b, nh, i = s
                    sp.wait_ge(xbias_done, n_xbias[a])
                    sp.dma_start(out[b].rearrange("(t p) d -> p t d", p=P)
                                 [:, 2 * i:2 * i + 2, nh * HALF:(nh + 1) * HALF],
                                 x[:, b * TT + 2 * i:b * TT + 2 * i + 2, nh * HALF:(nh + 1) * HALF]
                                 ).then_inc(stored, 16)
                    stores += 1
            sp.wait_ge(stored, 16 * stores)

        @block.gpsimd
        def _(pool):
            chain = [0]

            def link(ins):
                chain[0] += 1
                ins.then_inc(pool_chain, 1)
                pool.wait_ge(pool_chain, chain[0])

            link(pool.memset(ident[:, :], 0.0))
            pool.affine_select(out=ident[:, :], in_=ident[:, :], compare_op=ALU.not_equal, fill=1.0,
                               base=0, pattern=[[-1, P]], channel_multiplier=1).then_inc(consts_made, 1)
            link(pool.memset(ident16[:, :], 0.0))
            pool.affine_select(out=ident16[:, :], in_=ident16[:, :], compare_op=ALU.not_equal, fill=1.0,
                               base=0, pattern=[[-1, P]], channel_multiplier=1).then_inc(consts_made, 1)
            link(pool.memset(causal[:, :], 0.0))
            pool.affine_select(out=causal[:, 512 - P:], in_=causal[:, 512 - P:], compare_op=ALU.is_ge,
                               fill=LOWEST, base=0, pattern=[[-1, P]], channel_multiplier=1
                               ).then_inc(consts_made, 1)
            for s in GP:
                kind = s[0]
                if kind == "wlo":
                    c = s[1]
                    pool.wait_ge(whi_done, n_whi[c])
                    pool.tensor_tensor(w_lo[:, c % SPLIT, :], w_raw[:, c % RAW, :],
                                       w_hi[:, c % SPLIT, :].bitcast(F32), ALU.subtract
                                       ).then_inc(split_done, 1)
                elif kind == "qlo":
                    n = s[1]
                    pool.wait_ge(qmid_done, n_qmid[n])
                    pool.tensor_tensor(qk_parts[:, n % 2, 2, :], rest[:, :], qk_parts[:, n % 2, 1, :],
                                      ALU.subtract).then_inc(qlo_done, 1)
                elif kind == "vres":
                    _, a, l, b, part, i = s
                    pool.wait_ge(vhi_done, n_vhi[a])
                    pool.tensor_tensor(v_like(rest[:, :], l), v_like(rest[:, :], l),
                                      v_view(l, b, part, i, 0), ALU.subtract).then_inc(vres_done, 1)
                elif kind == "vlo":
                    _, a, l, b, part, i = s
                    pool.wait_ge(vmid_done, n_vmid[a])
                    pool.tensor_tensor(v_view(l, b, part, i, 2), v_like(rest[:, :], l),
                                      v_view(l, b, part, i, 1), ALU.subtract).then_inc(vlo_done, 1)
                elif kind == "msplit":
                    u = s[1]
                    pool.wait_ge(smax_done, last_smax[u])
                    if u >= 2:
                        pool.wait_ge(ring_made, mt_of[u - 2])
                    if u:
                        pool.wait_ge(msplit_done, n_msplit[u - 1])
                    mp = m_parts[:, u % 2, :, :]
                    link(pool.tensor_scalar(m_rest[:, :], maxima[:, u % 2, :], -1.0, None, ALU.mult))
                    link(pool.tensor_copy(mp[:, 0, :], m_rest[:, :]))
                    link(pool.tensor_tensor(m_rest[:, :], m_rest[:, :], mp[:, 0, :], ALU.subtract))
                    link(pool.tensor_copy(mp[:, 1, :], m_rest[:, :]))
                    pool.tensor_tensor(mp[:, 2, :], m_rest[:, :], mp[:, 1, :], ALU.subtract
                                       ).then_inc(msplit_done, 1)
                elif kind == "xbias":
                    _, a, l, b, nh, i = s
                    pool.wait_ge(acc_freed, n_acc_free[a])
                    pool.wait_ge(bo_here, 16 * (l + 1))
                    at = slice(b * TT + 2 * i, b * TT + 2 * i + 2)
                    dst = x[:, at, nh * HALF:(nh + 1) * HALF]
                    bias = bo_all[:, nh * HALF:(nh + 1) * HALF].unsqueeze(1).to_broadcast([P, 2, HALF])
                    pool.tensor_tensor(dst, dst, bias, ALU.add).then_inc(xbias_done, 1)
                else:
                    _, j, i = s
                    pool.wait_ge(exp_done, n_exp[j])
                    view = p32[:, j % 2, :]
                    if i in (0, 2):
                        view, n = view[:, 0:P], 1
                    elif i in (1, 3):
                        view, n = view.rearrange("p (b t) -> p b t", b=4)[:, 0:4:3, :], 2
                    else:
                        view, n = view.rearrange("p (b t) -> p b t", b=4)[:, 0:4:2, :], 2
                    pool.affine_select(out=view, in_=view, compare_op=ALU.is_ge, fill=0.0, base=0,
                                       pattern=[[0, n], [1, P]] if n == 2 else [[1, P]],
                                       channel_multiplier=-1).then_inc(mask_done, 1)

        @block.scalar
        def _(act):
            for s in SE:
                kind = s[0]
                if kind == "exp":
                    _, r, j, i = s
                    act.wait_ge(ring_made, n_ring[r])
                    if j >= 2:
                        act.wait_ge(plo_done, n_plo[j - 2])
                    act.activation(p32[:, j % 2, :], s_ring[r % SRING][:, :], ACT.Exp, scale=SCALE
                                   ).then_inc(exp_done, 1)
                elif kind == "whi":
                    c = s[1]
                    act.wait_ge(raw_here[c % RAW], 16 * (c // RAW + 1))
                    if c >= SPLIT:
                        act.wait_ge(work_done, n_chunk_used[c - SPLIT])
                    act.activation(w_hi[:, c % SPLIT, :], w_raw[:, c % RAW, :], ACT.Copy).then_inc(whi_done, 1)
                elif kind == "phi":
                    j = s[1]
                    act.wait_ge(mask_done, n_mask[j])
                    if j >= PRING:
                        act.wait_ge(pv_done, n_pv[(j - PRING) // 5])
                    act.activation(p_hi[:, j % PRING, :], p32[:, j % 2, :], ACT.Copy).then_inc(phi_done, 1)
                elif kind == "tanh":
                    _, n, g, m = s
                    act.wait_ge(work_done, n_g_made[g])
                    if n >= 2:
                        act.wait_ge(g_freed, hmul_of_gate[n - 2])
                    act.activation(gate[0:m, n % 2, :], g_ring[g % 2][0:m, :], ACT.Tanh, scale=0.5
                                   ).then_inc(tanh_done, 1)
                elif kind in ("xhi", "chi"):
                    g = s[1]
                    act.wait_ge(work_done, n_g_made[g])
                    if x_last_read[g] is not None:
                        act.wait_ge(work_done, x_last_read[g])
                    ps = g_ring[g % 2][:, :].rearrange("p (k t) -> p k t", k=KT)
                    if kind == "chi":
                        act.activation(xt_hi[:, s[2], s[3], :], g_ring[g % 2][:, :], ACT.Copy
                                       ).then_inc(xhi_done, 1)
                    else:
                        _, _, what, slot, tt = s
                        dst = xt_hi[:, slot, :, tt * P:(tt + 1) * P]
                        if what == "n":
                            act.wait_ge(consts_here, 48)
                        if what == "x":
                            act.activation(dst, ps, ACT.Copy).then_inc(xhi_done, 1)
                        else:
                            for kt in range(KT):
                                last = act.activation(dst[:, kt, :], ps[:, kt, :], ACT.Copy,
                                                      scale=lnw[:, kt:kt + 1])
                            last.then_inc(xhi_done, 1)
                elif kind == "qhi":
                    _, n, g, what, l, m = s
                    act.wait_ge(work_done, n_g_made[g])
                    if n >= 2:
                        act.wait_ge(qk_out[n % 2], 16 * (n // 2))
                    if n == 0:
                        act.wait_ge(consts_here, 48)
                    act.activation(qk_parts[:, n % 2, 0, :], g_ring[g % 2][:, :], ACT.Identity,
                                   bias=biases[:, l, "qk".index(what), m:m + 1]).then_inc(qhi_done, 1)
                elif kind == "qmid":
                    n = s[1]
                    act.wait_ge(g_freed, n_g_free[qk_g[n]])
                    act.activation(qk_parts[:, n % 2, 1, :], rest[:, :], ACT.Copy).then_inc(qmid_done, 1)
                elif kind == "vhi":
                    _, a, l, b, part, i = s
                    act.wait_ge(acc_freed, n_acc_free[a])
                    if v_before[(l, b)] is not None:
                        act.wait_ge(pv_done, v_before[(l, b)])
                    act.activation(v_view(l, b, part, i, 0), v_like(rest[:, :], l), ACT.Copy
                                   ).then_inc(vhi_done, 1)
                elif kind == "vmid":
                    _, a, l, b, part, i = s
                    act.wait_ge(vres_done, n_vres[a])
                    act.activation(v_view(l, b, part, i, 1), v_like(rest[:, :], l), ACT.Copy
                                   ).then_inc(vmid_done, 1)
                elif kind == "hhi":
                    _, hs, f, rows = s
                    act.wait_ge(g_freed, last_hmul[hs])
                    if hs >= HSPLIT:
                        act.wait_ge(work_done, n_out_used[hs - HSPLIT])
                    act.activation(h_hi[0:rows, hs % HSPLIT, :], h[0:rows, f, :], ACT.Copy
                                   ).then_inc(hhi_done, 1)
                elif kind == "root":
                    _, l, b = s
                    act.wait_ge(stats_done, n_stats[("stats", l, b)])
                    act.activation(root[:, :], ve[:, :], ACT.Sqrt).then_inc(root_done, 1)
                elif kind == "root2":
                    _, l, b = s
                    act.wait_ge(stats_done, n_stats[("rstd", l, b)])
                    act.activation(root2[:, :], ms[:, :], ACT.Sqrt).then_inc(root_done, 1)
                else:
                    raise AssertionError(kind)

        @block.vector
        def _(dve):
            chain = [0]

            def link(ins):
                chain[0] += 1
                ins.then_inc(dve_chain, 1)
                dve.wait_ge(dve_chain, chain[0])
                return chain[0]

            def inverse_root(dst, value, rooted):
                link(dve.reciprocal(dst, rooted))
                link(dve.tensor_tensor(newton[:, :], dst, dst, ALU.mult))
                link(dve.tensor_tensor(newton[:, :], newton[:, :], value, ALU.mult))
                link(dve.tensor_scalar(newton[:, :], newton[:, :], -0.5, 1.5, ALU.mult, ALU.add))
                return dve.tensor_tensor(dst, dst, newton[:, :], ALU.mult)

            dve.memset(k_op[QROWS:MROWS, :, :, :], 1.0)
            dve.memset(v_op[:, :, :, :, 3 * HD:3 * HD + 1].rearrange("p s t h c -> p (s t h) c"), 1.0
                       ).then_inc(ones_made, 1)
            for s in VE:
                kind = s[0]
                if kind == "stats":
                    _, l, b = s
                    if l == 1:
                        dve.wait_ge(xbias_done, x_final[(0, b)])
                    for tt in range(TT):
                        if l == 0:
                            dve.wait_ge(x_here[b * TT + tt], 16)
                        last = dve.bn_stats(bn[:, tt, :], x[:, b * TT + tt, :])
                    link(last)
                    for tt in range(TT):
                        last = dve.bn_aggr(mv[:, b, tt, :], bn[:, tt, :])
                    link(last)
                    dve.tensor_scalar(ve[:, :], mv[:, b, :, 1], EPS, None, ALU.add).then_inc(stats_done, 1)
                elif kind == "rstd":
                    _, l, b = s
                    dve.wait_ge(root_done, n_root[("root", l, b)])
                    if l == 1:
                        inverse_root(rstd[:, b, :], ve[:, :], root[:, :]).then_inc(stats_done, 1)
                    else:
                        link(inverse_root(rstd[:, b, :], ve[:, :], root[:, :]))
                        link(dve.tensor_tensor(ms[:, :], rstd[:, b, :], rstd[:, b, :], ALU.mult))
                        link(dve.tensor_tensor(ms[:, :], ms[:, :], mv[:, b, :, 1], ALU.mult))
                        dve.tensor_scalar(ms[:, :], ms[:, :], EPS, None, ALU.add).then_inc(stats_done, 1)
                elif kind == "rstd2":
                    _, l, b = s
                    dve.wait_ge(root_done, n_root[("root2", l, b)])
                    link(inverse_root(rstd_n[:, b, :], ms[:, :], root2[:, :]))
                    dve.tensor_tensor(rstd_n[:, b, :], rstd_n[:, b, :], rstd[:, b, :], ALU.mult
                                      ).then_inc(stats_done, 1)
                elif kind == "xn":
                    _, l, b, what, tt, g = s
                    n = n_xn[g]
                    dve.wait_ge(stats_done, n_stats[("rstd2" if what == "n" else "rstd", l, b)])
                    if n >= 2:
                        dve.wait_ge(work_done, xtr_made[n - 1])
                    scale = rstd if what == "x" else rstd_n
                    dve.tensor_scalar(xn[:, :], x[:, b * TT + tt, :], mv[:, b, tt, 0:1],
                                      scale[:, b, tt:tt + 1], ALU.subtract, ALU.mult).then_inc(xn_done, 1)
                elif kind in ("xlo", "clo"):
                    g = s[1]
                    dve.wait_ge(xhi_done, n_xhi[g])
                    ps = g_ring[g % 2][:, :].rearrange("p (k t) -> p k t", k=KT)
                    if kind == "clo":
                        dve.tensor_tensor(xt_lo[:, s[2], s[3], :], g_ring[g % 2][:, :],
                                          xt_hi[:, s[2], s[3], :].bitcast(F32), ALU.subtract
                                          ).then_inc(g_freed, 1)
                    else:
                        _, _, what, slot, tt = s
                        hi = xt_hi[:, slot, :, tt * P:(tt + 1) * P].bitcast(F32)
                        lo = xt_lo[:, slot, :, tt * P:(tt + 1) * P]
                        if what == "n":
                            dve.wait_ge(consts_here, 48)
                        if what == "x":
                            dve.tensor_tensor(lo, ps, hi, ALU.subtract).then_inc(g_freed, 1)
                        else:
                            for kt in range(KT):
                                last = dve.scalar_tensor_tensor(
                                    out=lo[:, kt, :], in0=ps[:, kt, :], scalar=lnw[:, kt:kt + 1],
                                    in1=hi[:, kt, :], op0=ALU.mult, op1=ALU.subtract)
                            last.then_inc(g_freed, 1)
                elif kind == "qres":
                    _, n, g, what, l, m = s
                    dve.wait_ge(qhi_done, n_qhi[n])
                    if n == 0:
                        dve.wait_ge(consts_here, 48)
                    if rest_before[s] is not None:
                        dve.wait_ge(*rest_before[s])
                    dve.scalar_tensor_tensor(
                        out=rest[:, :], in0=g_ring[g % 2][:, :],
                        scalar=biases[:, l, "qk".index(what), m:m + 1], in1=qk_parts[:, n % 2, 0, :],
                        op0=ALU.add, op1=ALU.subtract).then_inc(g_freed, 1)
                elif kind == "vsum":
                    _, a, l, b, part, i = s
                    dve.wait_ge(work_done, n_acc_made[a])
                    if rest_before[s] is not None:
                        dve.wait_ge(*rest_before[s])
                    if l == 0:
                        dve.tensor_copy(rest[:, :], acc[a % 2][:, :]).then_inc(acc_freed, 1)
                    else:
                        for t in range(2):
                            last = dve.tensor_tensor(
                                rest[:, t * HALF:(t + 1) * HALF], acc[a % 2][:, t * HALF:(t + 1) * HALF],
                                bv_all[:, part * HALF:(part + 1) * HALF], ALU.add)
                        last.then_inc(acc_freed, 1)
                elif kind == "gsum":
                    _, n, g, m = s
                    dve.wait_ge(tanh_done, n_tanh[n])
                    dve.scalar_tensor_tensor(
                        out=gate[0:m, n % 2, :], in0=gate[0:m, n % 2, :], scalar=1.0,
                        in1=g_ring[g % 2][0:m, :], op0=ALU.add, op1=ALU.mult).then_inc(g_freed, 1)
                elif kind == "hmul":
                    _, n, g, f, m = s
                    dve.wait_ge(g_freed, gsum_of_gate[n])
                    dve.wait_ge(work_done, n_g_made[g])
                    if f_before[s] is not None:
                        dve.wait_ge(*f_before[s])
                    dve.scalar_tensor_tensor(
                        out=h[0:m, f, :], in0=gate[0:m, n % 2, :], scalar=0.5,
                        in1=g_ring[g % 2][0:m, :], op0=ALU.mult, op1=ALU.mult).then_inc(g_freed, 1)
                elif kind == "hlo":
                    _, hs, f, rows = s
                    dve.wait_ge(hhi_done, n_hhi[hs])
                    dve.tensor_tensor(h_lo[0:rows, hs % HSPLIT, :], h[0:rows, f, :],
                                      h_hi[0:rows, hs % HSPLIT, :].bitcast(F32), ALU.subtract
                                      ).then_inc(hlo_done, 1)
                elif kind == "xadd":
                    _, a, l, b, nh, i = s
                    dve.wait_ge(work_done, n_acc_made[a])
                    at = slice(b * TT + 2 * i, b * TT + 2 * i + 2)
                    dst = x[:, at, nh * HALF:(nh + 1) * HALF]
                    dve.tensor_tensor(dst, acc[a % 2][:, :].rearrange("p (t n) -> p t n", t=2), dst,
                                      ALU.add).then_inc(acc_freed, 1)
                elif kind == "smax":
                    _, r, u, i = s
                    dve.wait_ge(ring_made, n_ring[r])
                    if i == 0 and u == 0:
                        dve.wait_ge(consts_made, 3)
                    if i == 0 and u >= 2:
                        dve.wait_ge(msplit_done, n_msplit[u - 2])
                    if i in (0, 2):
                        parts = ((i // 2, 3, 0),)
                    elif i in (1, 3):
                        parts = ((i // 2, 2, 0), (i // 2, 0, 3 * P))
                    else:
                        parts = ((0, 1, 0), (1, 1, 2 * P))
                    for j, qt, at in parts:
                        n = (qt + 1) * P
                        last = dve.tensor_tensor_reduce(
                            out=s_ring[r % SRING][:, at:at + n], in0=s_ring[r % SRING][:, at:at + n],
                            in1=causal[:, 512 - n:], scale=1.0, scalar=LOWEST, op0=ALU.add, op1=ALU.max,
                            accum_out=maxima[:, u % 2, j * 4 + qt:j * 4 + qt + 1])
                    last.then_inc(smax_done, 1)
                elif kind == "mrow":
                    _, r, u = s
                    dve.wait_ge(ring_made, n_ring[r])
                    if u >= 2:
                        dve.wait_ge(m_out[u % 2], 16 * (u // 2))
                    dve.tensor_copy(m_rows[:, u % 2, :], s_ring[r % SRING][:, :].bitcast(BF16)[0:24, 0:P]
                                    ).then_inc(smax_done, 1)
                elif kind == "plo":
                    j = s[1]
                    dve.wait_ge(phi_done, n_phi[j])
                    dve.tensor_tensor(p_lo[:, j % PRING, :], p32[:, j % 2, :], p_hi[:, j % PRING, :],
                                      ALU.subtract).then_inc(plo_done, 1)
                elif kind == "norm":
                    u = s[1]
                    dve.wait_ge(pv_done, n_pv[u])
                    if u % PAIRS == 0 and u:
                        dve.wait_ge(work_done, ctx_used[u // PAIRS - 1])
                    sums = pv_ps[:, 0:8 * VW].rearrange("p (g c) -> p g c", c=VW)
                    link(dve.reduce_sum(pv_sum[:, :, :, :].rearrange("p q j d -> p (q j) d"),
                                        sums[:, :, 0:3 * HD].rearrange("p g (s d) -> p g d s", s=3), AX))
                    link(dve.reciprocal(recip[:, :, :].rearrange("p q j -> p (q j)"), sums[:, :, 3 * HD]))
                    c0 = (u % PAIRS) * 2 * HD
                    dve.tensor_tensor(
                        context[:, :, c0:c0 + 2 * HD].rearrange("p q (j d) -> p q j d", j=2),
                        pv_sum[:, :, :, :], recip[:, :, :].unsqueeze(3).to_broadcast([P, TT, 2, HD]),
                        ALU.mult).then_inc(norm_done, 1)
                else:
                    raise AssertionError(kind)

        @block.tensor
        def _(pe):
            def three_passes(dst, w, xa, first, last, skip=False):
                for i, (a, c) in enumerate(((0, 0), (0, 1), (1, 0))):
                    ins = pe.matmul(dst, w[a], xa[c], start=first and i == 0, stop=last and i == 2,
                                    skip_group_check=skip)
                return ins

            def wait_g(g):
                if g >= 2:
                    pe.wait_ge(g_freed, n_g_free[g - 2])

            def wait_ring(r):
                if r >= SRING:
                    old = ring_step[r - SRING]
                    if old[0] == "T":
                        pe.wait_ge(exp_done, exp_of_ring[r - SRING])
                    else:
                        pe.wait_ge(smax_done, n_smax[r - SRING])

            def wait_acc(a):
                if a >= 2:
                    pe.wait_ge(acc_freed, n_acc_free[a - 2])

            pe.wait_ge(consts_made, 2)
            for s in PE:
                kind = s[0]
                if kind == "xtr":
                    _, g, l, b, what, tt = s
                    wait_g(g)
                    pe.wait_ge(xn_done, n_xn[g])
                    for kt in range(KT):
                        last = pe.transpose(g_ring[g % 2][:, kt * P:(kt + 1) * P],
                                            xn[:, kt * P:(kt + 1) * P], ident[:, :])
                    last.then_inc(work_done, 1)
                elif kind == "ctr":
                    _, g, kt = s
                    wait_g(g)
                    phase = ctrs.index(s) // KT
                    pe.wait_ge(norm_done, n_norm[PAIRS * phase + PAIRS - 1])
                    for tt in range(TT):
                        last = pe.transpose(g_ring[g % 2][:, tt * P:(tt + 1) * P],
                                            context[:, tt, kt * P:(kt + 1) * P], ident[:, :])
                    last.then_inc(work_done, 1)
                elif kind == "proj":
                    _, c, g, slot, m = s
                    wait_g(g)
                    pe.wait_ge(split_done, n_split[c])
                    pe.wait_ge(g_freed, x_free_count[s])
                    for kt in range(KT):
                        w = [t[:, c % SPLIT, kt * P:kt * P + m] for t in (w_hi, w_lo)]
                        xa = [t[:, slot, kt, :] for t in (xt_hi, xt_lo)]
                        last = three_passes(g_ring[g % 2][0:m, :], w, xa, kt == 0, kt == KT - 1)
                    last.then_inc(work_done, 1)
                elif kind == "v0":
                    _, c, a, slot = s
                    wait_acc(a)
                    pe.wait_ge(split_done, n_split[c])
                    pe.wait_ge(g_freed, x_free_count[s])
                    for tt in range(TT):
                        for kt in range(KT):
                            w = [t[:, slot, kt, tt * P:(tt + 1) * P] for t in (xt_hi, xt_lo)]
                            xa = [t[:, c % SPLIT, kt * P:(kt + 1) * P] for t in (w_hi, w_lo)]
                            last = three_passes(acc[a % 2][:, tt * P:(tt + 1) * P], w, xa, kt == 0,
                                                kt == KT - 1)
                    last.then_inc(work_done, 1)
                elif kind in ("v1", "out"):
                    if kind == "v1":
                        _, c, a, slot, i = s
                        tiles, first, last_step, rows = (2 * i, 2 * i + 1), i == 0, i == 1, P
                        end = True
                    else:
                        _, c, a, slot, kt, hs, i, rows, first, last_step, end = s
                        tiles = (kt,)
                    if first:
                        wait_acc(a)
                        wait_acc(a + 1)
                    pe.wait_ge(split_done, n_split[c])
                    if s in x_free_count:
                        pe.wait_ge(g_freed, x_free_count[s])
                    if kind == "out" and hs >= 0:
                        pe.wait_ge(hlo_done, n_hlo[hs])
                    for n, kt in enumerate(tiles):
                        col = (n if kind == "v1" else i) * HALF
                        xa = [t[0:rows, c % SPLIT, col:col + HALF] for t in (w_hi, w_lo)]
                        for tt in range(TT):
                            at = slice(tt * P, (tt + 1) * P)
                            if kt >= 0:
                                w = [t[0:rows, slot, kt, at] for t in (xt_hi, xt_lo)]
                            else:
                                w = [t[0:rows, hs % HSPLIT, at] for t in (h_hi, h_lo)]
                            bank = (a + tt // 2) % 2
                            last = three_passes(acc[bank][:, tt % 2 * HALF:(tt % 2 + 1) * HALF], w, xa,
                                                first and n == 0 and tt % 2 == 0,
                                                last_step and n == len(tiles) - 1, skip=True)
                            if last_step and n == len(tiles) - 1 and tt == 1:
                                last.then_inc(work_done, 1)
                    last.then_inc(work_done, 1)
                elif kind == "S":
                    _, r, u, i = s
                    wait_ring(r)
                    if i == 0:
                        octet = u // 4
                        pe.wait_ge(q_here[octet % 2], arrival[("q", octet)])
                        pe.wait_ge(k_here[k_slot_and_head(u, 0)[0]], arrival[("k", octet)])
                    if i in (0, 2):
                        parts = ((i // 2, 3, 0),)
                    elif i in (1, 3):
                        parts = ((i // 2, 2, 0), (i // 2, 0, 3 * P))
                    else:
                        parts = ((0, 1, 0), (1, 1, 2 * P))
                    for j, qt, at in parts:
                        n = (qt + 1) * P
                        ks, kh = k_slot_and_head(u, j)
                        last = pe.matmul(s_ring[r % SRING][:, at:at + n],
                                         q_op[0:QROWS, u // 4 % 2, 2 * (u % 4) + j, qt * P:(qt + 1) * P],
                                         k_op[0:QROWS, ks, kh, 0:n], start=True, stop=True)
                    last.then_inc(ring_made, 1)
                elif kind == "Mt":
                    _, r, u = s
                    wait_ring(r)
                    pe.wait_ge(msplit_done, n_msplit[u])
                    pe.transpose(s_ring[r % SRING][:, :].bitcast(BF16)[0:24, 0:P],
                                 m_parts[:, u % 2, :, :].rearrange("p s g -> p (s g)"), ident16[:, :]
                                 ).then_inc(ring_made, 1)
                elif kind == "T":
                    _, r, j_no, u, i = s
                    wait_ring(r)
                    if u == 0 and i == 0:
                        pe.wait_ge(ones_made, 1)
                    if i == 0:
                        pe.wait_ge(m_here[u % 2], 16 * (u // 2 + 1))
                    if i in (0, 2):
                        parts = ((i // 2, 0, 0),)
                    elif i in (1, 3):
                        parts = ((i // 2, 1, 0), (i // 2, 3, 3 * P))
                    else:
                        parts = ((0, 2, 0), (1, 2, 2 * P))
                    for j, kt, at in parts:
                        n = T - kt * P
                        ks, kh = k_slot_and_head(u, j)
                        last = pe.matmul(s_ring[r % SRING][:, at:at + n],
                                         k_op[0:MROWS, ks, kh, kt * P:(kt + 1) * P],
                                         q_op[0:MROWS, u // 4 % 2, 2 * (u % 4) + j, kt * P:T],
                                         start=True, stop=True)
                    last.then_inc(ring_made, 1)
                elif kind == "PV":
                    _, u, half = s
                    l, b = PHASES[u // PAIRS]
                    if half == 0:
                        if u % PAIRS == 0:
                            pe.wait_ge(vlo_done, vlo_at[(0, 1) if l == 0 else (1, b)])
                        if u:
                            pe.wait_ge(norm_done, n_norm[u - 1])
                        pe.wait_ge(plo_done, n_plo[5 * u + 4])
                    j = half
                    slot, vh = v_head(u, j)
                    for qt in range(TT):
                        dst = pv_ps[:, (qt * 2 + j) * VW:(qt * 2 + j) * VW + 3 * HD + 1]
                        for kt in range(qt + 1):
                            job, at = ((2 * j, qt * P), (2 * j + 1, (qt - 1) * P),
                                       (4, 2 * P * j + (qt - 2) * P), (2 * j + 1, 3 * P))[kt]
                            ring = (5 * u + job) % PRING
                            for n, part in enumerate((p_hi, p_lo)):
                                last = pe.matmul(dst, part[:, ring, at:at + P],
                                                 v_op[:, slot, kt, vh, 0:3 * HD + 1],
                                                 start=kt == 0 and n == 0, stop=kt == qt and n == 1)
                    if half == 1:
                        last.then_inc(pv_done, 1)
                else:
                    raise AssertionError(kind)


def chunks_of(w, cols, tiles):
    k, n = w.shape
    rows = -(-k // (P * tiles)) * P * tiles
    wide = -(-n // cols) * cols
    full = np.zeros((rows, wide), w.dtype)
    full[:k, :n] = w
    c = full.reshape(rows // (P * tiles), tiles, P, wide // cols, cols)
    return c.transpose(3, 0, 2, 1, 4).reshape(-1, P, 512)


def pack_weights(w):
    wkv = w["L0_attn_Wkv"].reshape(D, G, 2, HD)
    layers = (
        (w["L0_attn_Wq"], wkv[:, :, 0].reshape(D, G * HD), wkv[:, :, 1].reshape(D, G * HD),
         w["L0_ffn_gate_w"].T, w["L0_ffn_up_w"].T, w["L0_attn_Wo"], w["L0_ffn_down_w"].T),
        (w["L1_attn_Wq"].T, w["L1_attn_Wk"].T, w["L1_attn_Wv"].T,
         w["L1_ffn_W_gate"].T, w["L1_ffn_W_up"].T, w["L1_attn_Wo"].T, w["L1_ffn_W_down"].T),
    )
    parts = []
    for l, (q, k, v, gate, up, o, down) in enumerate(layers):
        parts += [chunks_of(q, P, KT), chunks_of(k, P, KT)]
        parts.append(chunks_of(v, P, KT) if l == 0 else chunks_of(v, HALF, 2))
        both = np.stack([chunks_of(gate, P, KT), chunks_of(up, P, KT)], axis=1)
        parts.append(both.reshape(-1, P, 512))
        parts += [chunks_of(o, HALF, 2), chunks_of(down, HALF, 2)]
    return np.ascontiguousarray(np.concatenate(parts))


def kernel(**inputs):
    import concourse.bacc as bacc
    from concourse.bass_utils import run_bass_kernel_spmd

    w = {k: np.asarray(v) for k, v in inputs.items()}
    qk_bias = np.zeros((P, 2, 2, 4), np.float32)
    qk_bias[:, 1, 0] = w["L1_attn_bq"].reshape(4, P).T
    qk_bias[:, 1, 1] = w["L1_attn_bk"].reshape(4, P).T
    arrays = {
        "x": np.ascontiguousarray(w["L0_attn_x"]),
        "weights": pack_weights(w),
        "qk_bias": qk_bias,
        "ln_w": np.ascontiguousarray(w["L0_ffn_ln_w"].reshape(KT, P).T),
        "bv": np.ascontiguousarray(w["L1_attn_bv"]),
        "bo0": np.ascontiguousarray(w["L0_attn_bo"]),
        "bo1": np.ascontiguousarray(w["L1_attn_bo"]),
    }
    nc = bacc.Bacc("TRN2", target_bir_lowering=False, num_devices=1)
    args = [nc.dram_tensor(f"{n}_in", a.shape, F32, kind="ExternalInput").ap() for n, a in arrays.items()]
    qk_scratch = nc.dram_tensor("qk_scratch", (2, P, 3, T), BF16).ap()
    m_scratch = nc.dram_tensor("m_scratch", (2, 24, P), BF16).ap()
    out = nc.dram_tensor("y_out", (B, T, D), F32, kind="ExternalOutput").ap()
    two_layers(nc, *args, qk_scratch, m_scratch, out)
    got = run_bass_kernel_spmd(nc, [{f"{n}_in": a for n, a in arrays.items()}], core_ids=[0])
    return got.results[0]["y_out"]
```
